# Optimizing a Trainium2 kernel written in Bass

```python
import numpy as np
import jax
import jax.numpy as jnp

def _softmax(x, axis=-1):
    return jax.nn.softmax(x, axis=axis)

def _gelu(x):
    return jax.nn.gelu(x, approximate=True)

def _silu(x):
    return jax.nn.silu(x)

def _sigmoid(x):
    return jax.nn.sigmoid(x)

def _layernorm(x, axis=-1, eps=1e-05):
    m = jnp.mean(x, axis=axis, keepdims=True)
    v = jnp.var(x, axis=axis, keepdims=True)
    return (x - m) / jnp.sqrt(v + eps)

def _scatter_add(tgt, idx, src, axis=0):
    return tgt.at[idx].add(src)

def _segment_sum(src, seg, n):
    return jax.ops.segment_sum(src, seg, n)
kernel_name = 'mk_adaln_d1_jaxref_r8_271a69'

def setup_inputs(seed: int=0):
    np.random.seed(seed)
    _w = jnp.asarray

    def _L0_attn_setup():
        import jax, jax.numpy as jnp
        import numpy as np
        HIDDEN, KEY_DIM, VALUE_DIM = (128, 128, 128)
        BATCH, SEQ = (8, 256)
        key = jax.random.key(seed)
        ks = jax.random.split(key, 9)
        s = lambda fan_in: 1.0 / np.sqrt(fan_in)
        return {'y_all': jax.random.normal(ks[0], (BATCH, SEQ, HIDDEN), dtype=jnp.float32), 'Wq': jax.random.uniform(ks[1], (HIDDEN, KEY_DIM), jnp.float32, -s(HIDDEN), s(HIDDEN)), 'bq': jax.random.uniform(ks[2], (KEY_DIM,), jnp.float32, -s(HIDDEN), s(HIDDEN)), 'Wk': jax.random.uniform(ks[3], (HIDDEN, KEY_DIM), jnp.float32, -s(HIDDEN), s(HIDDEN)), 'bk': jax.random.uniform(ks[4], (KEY_DIM,), jnp.float32, -s(HIDDEN), s(HIDDEN)), 'Wv': jax.random.uniform(ks[5], (HIDDEN, VALUE_DIM), jnp.float32, -s(HIDDEN), s(HIDDEN)), 'bv': jax.random.uniform(ks[6], (VALUE_DIM,), jnp.float32, -s(HIDDEN), s(HIDDEN)), 'Wo': jax.random.uniform(ks[7], (VALUE_DIM, HIDDEN), jnp.float32, -s(VALUE_DIM), s(VALUE_DIM)), 'bo': jax.random.uniform(ks[8], (HIDDEN,), jnp.float32, -s(VALUE_DIM), s(VALUE_DIM))}
    _L0_attn_in = _L0_attn_setup()

    def _L0_ffn_setup():
        import jax, jax.numpy as jnp
        import numpy as np
        N_BLOCKS = 16
        BLOCK = 32
        TOP_K = N_BLOCKS // 4
        key = jax.random.key(seed)
        ks = jax.random.split(key, 7)
        D, H = (128, 512)
        s = lambda k, shape, scale: jax.random.normal(k, shape, dtype=jnp.float32) * scale
        return {'x': s(ks[0], (4, 512, D), 1.0), 'w_router': s(ks[1], (D, N_BLOCKS), 0.03), 'b_router': s(ks[2], (N_BLOCKS,), 0.01), 'w1': s(ks[3], (H, D), 0.03), 'b1': s(ks[4], (H,), 0.01), 'w2': s(ks[5], (D, H), 0.03), 'b2': s(ks[6], (D,), 0.01)}
    _L0_ffn_in = _L0_ffn_setup()
    _L0_c = _w((lambda *s: np.random.randn(*s).astype(np.float32) * 0.05)(1, 128))
    _L0_wmod = _w((lambda *s: np.random.randn(*s).astype(np.float32) * 0.05)(128, 6 * 128) * 128 ** (-0.5))
    _d = {'L0_attn_y_all': _L0_attn_in['y_all'], 'L0_attn_Wq': _L0_attn_in['Wq'], 'L0_attn_bq': _L0_attn_in['bq'], 'L0_attn_Wk': _L0_attn_in['Wk'], 'L0_attn_bk': _L0_attn_in['bk'], 'L0_attn_Wv': _L0_attn_in['Wv'], 'L0_attn_bv': _L0_attn_in['bv'], 'L0_attn_Wo': _L0_attn_in['Wo'], 'L0_attn_bo': _L0_attn_in['bo'], 'L0_ffn_w_router': _L0_ffn_in['w_router'], 'L0_ffn_b_router': _L0_ffn_in['b_router'], 'L0_ffn_w1': _L0_ffn_in['w1'], 'L0_ffn_b1': _L0_ffn_in['b1'], 'L0_ffn_w2': _L0_ffn_in['w2'], 'L0_ffn_b2': _L0_ffn_in['b2'], 'L0_c': _L0_c, 'L0_wmod': _L0_wmod}
    _x0 = _d['L0_attn_y_all']
    _d['L0_attn_y_all'] = jax.random.normal(jax.random.fold_in(jax.random.key(seed), 1), (1, 2048, 128), dtype=_x0.dtype)
    del _x0
    return _d

def reference(L0_attn_y_all, L0_attn_Wq, L0_attn_bq, L0_attn_Wk, L0_attn_bk, L0_attn_Wv, L0_attn_bv, L0_attn_Wo, L0_attn_bo, L0_ffn_w_router, L0_ffn_b_router, L0_ffn_w1, L0_ffn_b1, L0_ffn_w2, L0_ffn_b2, L0_c, L0_wmod):

    def _L0_attn_ref(y_all, Wq, bq, Wk, bk, Wv, bv, Wo, bo):
        import jax, jax.numpy as jnp
        import numpy as np
        HIDDEN, KEY_DIM, VALUE_DIM = (128, 128, 128)
        BATCH, SEQ = (8, 256)
        B, T, H = y_all.shape
        dk = Wq.shape[1]
        q = (y_all @ Wq + bq) / jnp.sqrt(jnp.asarray(dk, y_all.dtype))
        k = y_all @ Wk + bk
        v = y_all @ Wv + bv
        scores = jnp.einsum('bid,bjd->bij', q, k)
        causal = jnp.tril(jnp.ones((T, T), dtype=bool))
        scores = jnp.where(causal, scores, -jnp.inf)
        weights = jax.nn.softmax(scores, axis=-1)
        ctx = jnp.einsum('bij,bjd->bid', weights, v)
        return ctx @ Wo + bo

    def _L0_ffn_ref(x, w_router, b_router, w1, b1, w2, b2):
        import jax, jax.numpy as jnp
        import numpy as np
        N_BLOCKS = 16
        BLOCK = 32
        TOP_K = N_BLOCKS // 4
        orig_shape = x.shape
        D = orig_shape[-1]
        xf = x.reshape(-1, D)
        prob = jax.nn.softmax(xf @ w_router + b_router, axis=-1)
        _, idx = jax.lax.top_k(prob, TOP_K)
        mask = (idx[:, :, None] == jnp.arange(N_BLOCKS)[None, None, :]).any(axis=1)
        mask = mask.astype(x.dtype)
        w1b = w1.reshape(N_BLOCKS, BLOCK, D)
        b1b = b1.reshape(N_BLOCKS, BLOCK)
        w2b = jnp.transpose(w2.reshape(D, N_BLOCKS, BLOCK), (1, 2, 0))
        h = jax.nn.relu(jnp.einsum('nd,ebd->neb', xf, w1b) + b1b[None])
        y = jnp.einsum('neb,ebd,ne->nd', h, w2b, mask)
        y = y + b2[None, :]
        return y.reshape(orig_shape)
    x = L0_attn_y_all
    mod = (_silu(L0_c) @ L0_wmod).reshape(L0_c.shape[0], 6, 1, -1)
    sa, ca, ga, sb, cb, gb = (mod[:, 0], mod[:, 1], mod[:, 2], mod[:, 3], mod[:, 4], mod[:, 5])
    ga = (2 * (ga >= 0) - 1) * jnp.maximum(jnp.abs(ga), 0.25)
    gb = (2 * (gb >= 0) - 1) * jnp.maximum(jnp.abs(gb), 0.25)
    h = _layernorm(x, axis=-1) * (1 + ca) + sa
    x = x + ga * _L0_attn_ref(h, L0_attn_Wq, L0_attn_bq, L0_attn_Wk, L0_attn_bk, L0_attn_Wv, L0_attn_bv, L0_attn_Wo, L0_attn_bo)
    h = _layernorm(x, axis=-1) * (1 + cb) + sb
    x = x + gb * _L0_ffn_ref(h, L0_ffn_w_router, L0_ffn_b_router, L0_ffn_w1, L0_ffn_b1, L0_ffn_w2, L0_ffn_b2)
    return x

_drawn_inputs = setup_inputs


def setup_inputs(seed=0):
    import zlib

    import numpy as np

    out = dict(_drawn_inputs(seed))
    spreads = {}
    factors = {'L0_attn_Wq': 8.0,
     'L0_attn_bq': 8.0,
     'L0_attn_Wk': 8.0,
     'L0_attn_bk': 64.0,
     'L0_attn_Wv': 8.0,
     'L0_attn_bv': 6.54,
     'L0_attn_Wo': 5.838,
     'L0_attn_bo': 14.601,
     'L0_ffn_w_router': 3.256,
     'L0_ffn_b_router': 36.768,
     'L0_ffn_w1': 3.377,
     'L0_ffn_b1': 64.0,
     'L0_ffn_w2': 2.803,
     'L0_ffn_b2': 64.0}
    for name, (base, spread) in spreads.items():
        noise = np.random.default_rng([zlib.crc32(name.encode()), seed]).standard_normal(out[name].shape)
        drawn = base * np.exp(spread * noise) if base else spread * noise
        out[name] = jnp.asarray(drawn.astype(out[name].dtype))
    for name, factor in factors.items():
        out[name] = (out[name] * factor).astype(out[name].dtype)
    return out
```

```python
from contextlib import ExitStack

import concourse.bass as bass
from concourse import mybir

ALU = mybir.AluOpType
ACT = mybir.ActivationFunctionType
AX = mybir.AxisListType
F32 = mybir.dt.float32
F32R = mybir.dt.float32r
BF16 = mybir.dt.bfloat16


P = 128
GT = 4
GW = GT * P
EPS = 1e-5
FAR = -1e30
UNDER = -87.33


def adaln_attention_sparse_ffn(nc, x_in, wq_in, bq_in, wk_in, bk_in, wv_in, bv_in, wo_in, bo_in,
                               wr_in, br_in, w1_in, b1_in, w2_in, b2_in, c_in, wmod_in, out):
    _, T, D = x_in.shape
    HID = w1_in.shape[0]
    NBLK = wr_in.shape[1]
    TOPK = NBLK // 4
    BLK = HID // NBLK
    NT = T // P
    NG = T // GW
    NH = HID // P
    PADS = 8 - TOPK
    KEYS = NBLK + PADS
    QSCALE = float(D) ** -0.5
    assert D == P and wq_in.shape[1] == P and HID == GW and NG == 4

    def chunk_no(g, r, c):
        return sum(GT * (k + 1) for k in range(g)) + r * (g + 1) + c

    def chunk_width(g, r, c):
        return GW if c < g else P * (r + 1)

    def key_no(g, j):
        return sum(GT * (k + 1) for k in range(g)) + j

    def key_from(g, j):
        return max(0, j - GT * g)

    CHUNKS = chunk_no(NG, 0, 0)
    pt_cols = [P * key_from(g, j) for g in range(NG) for j in range(GT * (g + 1))]

    def pool_splits(t):
        return t % 3 == 1

    def splits_before(t, by_pool):
        return sum(pool_splits(k) == by_pool for k in range(t))

    def mix(g):
        js = list(range(GT * (g + 1)))
        cs = [(r, c) for r in range(GT) for c in range(g + 2)] if g + 1 < NG else []
        steps, done = [], 0
        aside = {}
        if g >= 1:
            first = 9 if g == NG - 1 else 3
            aside = {1: ("normalise", g - 1), first: ("turn norm", g - 1), first + 2: ("route", g - 1),
                     first + 4: ("mask", g - 1)}
        if g == NG - 1:
            aside |= {2 + 2 * m: ("hidden", m) for m in range(NH)}

        def key(j):
            return [("key", j)] + ([aside[j]] if j in aside else [])

        for n, rc in enumerate(cs):
            steps.append(("score", rc))
            upto = (n + 1) * len(js) // len(cs)
            for j in js[done:upto]:
                steps += key(j)
            done = upto
        for j in js[done:]:
            steps += key(j)
        return steps

    with ExitStack() as ctx:
        def sb(name, shape, dt=F32):
            return ctx.enter_context(nc.sbuf_tensor(name, shape, dt))

        def sem(name):
            return ctx.enter_context(nc.semaphore(name))

        bank = [ctx.enter_context(nc.psum_tensor(f"bank{i}", [P, GW], F32)) for i in range(8)]
        score_bank = bank[0:4]
        turn_bank = bank[4:6]
        ctx_bank, misc_bank = bank[6], bank[7]

        x = sb("x", [P, NT, D])
        x1 = x
        xn = sb("xn", [P, 2, GT, D])
        h_full = sb("h_full", [P, 2, GW])
        h_hi = sb("h_hi", [P, 2, GW], F32R)
        h_lo = sb("h_lo", [P, 2, GW], F32R)
        q_full = sb("q_full", [P, 2, GW])
        q_hi = sb("q_hi", [P, T], F32R)
        q_lo = sb("q_lo", [P, T], F32R)
        k_full = sb("k_full", [P, 2, GW])
        k_hi = sb("k_hi", [P, T], F32R)
        k_lo = sb("k_lo", [P, T], F32R)
        v_full = sb("v_full", [P, 2, GW])
        v_hi = sb("v_hi", [P, T], F32R)
        v_lo = sb("v_lo", [P, T], F32R)
        probs = [sb("probs0", [P, GT, 3 * GW]), sb("probs1", [P, GT, 4 * GW])]
        pt_full = sb("pt_full", [P, 2, GW])
        pt_hi = sb("pt_hi", [P, 3, GW], F32R)
        pt_lo = sb("pt_lo", [P, 3, GW], F32R)
        ctx_sb = q_full[:, 0, :]
        g_full, g_hi, g_lo = h_full, h_hi, h_lo
        hid_hi = sb("hid_hi", [P, NH, GW], F32R)
        hid_lo = sb("hid_lo", [P, NH, GW], F32R)
        y_sb = k_full[:, 0, :]
        res = v_full
        wq, wk, wv, wo = (sb(n, [P, P]) for n in ("wq", "wk", "wv", "wo"))
        wq_hi, wk_hi, u_hi = (sb(n, [P, P], F32R) for n in ("wq_hi", "wk_hi", "u_hi"))
        wq_lo, wk_lo, u_lo = (sb(n, [P, P], F32R) for n in ("wq_lo", "wk_lo", "u_lo"))
        wv_t = sb("wv_t", [P, P])
        u_full = sb("u_full", [P, P])
        bv_wide = sb("bv_wide", [P, P])
        bv_out = sb("bv_out", [P, P])
        gbo_wide = sb("gbo_wide", [P, P])
        gbo_row = sb("gbo_row", [P, P])
        w1 = probs[1][:, 0, 0:HID].rearrange("p (m d) -> p m d", m=NH)
        w2 = probs[1][:, 1, 0:HID]
        wmod = probs[1][:, 2, 0:6 * D]
        w1t_full = sb("w1t_full", [P, HID])
        w2t_full = sb("w2t_full", [P, HID])
        w1t_hi, w1t_lo = sb("w1t_hi", [P, HID], F32R), sb("w1t_lo", [P, HID], F32R)
        w2t_hi, w2t_lo = sb("w2t_hi", [P, HID], F32R), sb("w2t_lo", [P, HID], F32R)
        wr = sb("wr", [P, NBLK])
        br = sb("br", [P, GT, NBLK])
        cols = sb("cols", [P, 6])
        BQ, BK, BV, BO, B2, C = range(6)
        silu = sb("silu", [P, 4])
        mod = sb("mod", [P, 6])
        SA, CA, GA, SB_, CB, GB = range(6)
        gate = sb("gate", [P, 6])
        bqs = sb("bqs", [P, 1])
        gbb2 = sb("gbb2", [P, 1])
        ident = sb("ident", [P, P])
        ident_b = sb("ident_b", [P, P], BF16)
        causal = sb("causal", [P, P], BF16)
        pow_half = sb("pow_half", [P, GT])
        pick = sb("pick", [P, HID], BF16)
        pick_f = k_full[:, 1, :]
        route = sb("route", [P, T], BF16)
        b1 = sb("b1", [P, HID])
        b1_part = route[:, 0:HID]
        st = sb("st", [P, 2, NT, 6])
        mv = sb("mv", [P, 2, NT, 2])
        rstd = sb("rstd", [P, 2, NT])
        nmean = sb("nmean", [P, 2, NT])
        cmax = sb("cmax", [P, NT, NG])
        nmax = sb("nmax", [P, NT])
        dpart = sb("dpart", [P, NT, NG])
        den = sb("den", [P, NT])
        rden = sb("rden", [P, NT])
        logit = sb("logit", [P, GT, NBLK])
        lmax = sb("lmax", [P, GT])
        ldiff = sb("ldiff", [P, GT, NBLK])
        keys = sb("keys", [P, GT, KEYS])
        top8 = sb("top8", [P, GT, 8])
        marked = sb("marked", [P, GT, KEYS])
        nmask = sb("nmask", [P, GT, NBLK], BF16)

        x_in_s = [sem(f"x_loaded{g}") for g in range(NG)]
        mod_in_s, cols_in_s, wqk_in_s, wvo_in_s = (sem(n) for n in ("wmod_loaded", "cols_loaded", "wqk_loaded", "wvo_loaded"))
        ffn_in_s, b1_in_s = sem("ffn_weights_loaded"), sem("b1_loaded")
        stored = [sem(f"stored{g}") for g in range(NG)]
        consts_made, blank = sem("consts_made"), sem("blank")
        silu_e, mod_mm, mod_ready, wv_turned, wv_t_ready = (sem(n) for n in ("silu_exp", "mod_mm", "mod_ready", "wv_turned", "wv_t_ready"))
        u_mm, u_ready, gbo_mm, gbo_ready = (sem(n) for n in ("u_mm", "u_ready", "gbo_mm", "gbo_ready"))
        wide_ready, qk_w_ready = sem("wide_ready"), sem("qk_w_ready")
        w_turned, w_t_full, ffn_w_ready, pick_ready = (sem(n) for n in ("w_turned", "w_t_full", "ffn_w_ready", "pick_ready"))
        stats, xn_ready = sem("stats"), sem("xn_ready")
        dve_step, pool_step = sem("dve_step"), sem("pool_step")
        xt_mm, h_full_s, h_hi_s, h_lo_s = (sem(n) for n in ("xt_mm", "h_full_s", "h_hi_s", "h_lo_s"))
        q_mm, k_mm, v_mm = sem("q_mm"), sem("k_mm"), sem("v_mm")
        q_full_s, k_full_s, v_full_s = sem("q_full_s"), sem("k_full_s"), sem("v_full_s")
        q_hi_s, k_hi_s, v_hi_s = sem("q_hi_s"), sem("k_hi_s"), sem("v_hi_s")
        q_lo_s, k_lo_s, v_lo_s = sem("q_lo_s"), sem("k_lo_s"), sem("v_lo_s")
        xb_ready = sem("xb_ready")
        scored, nmax_ready, exp_done = sem("scored"), sem("nmax_ready"), sem("exp_done")
        turned, pt_full_s, pt_hi_act, pt_hi_dve = sem("turned"), sem("pt_full_s"), sem("pt_hi_act"), sem("pt_hi_dve")
        pt_lo_dve, pt_lo_pool, pv_done = sem("pt_lo_dve"), sem("pt_lo_pool"), sem("pv_done")
        rden_ready, ctx_out, ctx_turned, x1_ready = sem("rden_ready"), sem("ctx_out"), sem("ctx_turned"), sem("x1_ready")
        g_turned, g_full_s, g_hi_s, g_lo_s = sem("g_turned"), sem("g_full_s"), sem("g_hi_s"), sem("g_lo_s")
        logits_mm, logit_read, nmask_ready, nmask_turned, route_ready = (
            sem(n) for n in ("logits_mm", "logit_read", "nmask_ready", "nmask_turned", "route_ready"))
        hid_mm, hid_hi_s, hid_lo_s, y_mm, y_out, y_turned, res_ready = (
            sem(n) for n in ("hid_mm", "hid_hi_s", "hid_lo_s", "y_mm", "y_out", "y_turned", "res_ready"))

        x_tiles = x_in.rearrange("b (g i p) d -> g p (b i) d", p=P, i=GT)
        out_tiles = out.rearrange("b (g i p) d -> g p (b i) d", p=P, i=GT)
        col = lambda v: v.rearrange("(p o) -> p o", o=1)

        def grp(a, g):
            return a[:, g * GW:(g + 1) * GW]

        def tile(a, n):
            return a[:, n * P:(n + 1) * P]

        block = ctx.enter_context(nc.Block())

        @block.sync
        def _(sp):
            sp.dma_start(x[:, 0:GT, :], x_tiles[0]).then_inc(x_in_s[0], 16)
            sp.dma_start(wq[:], wq_in).then_inc(wqk_in_s, 16)
            sp.dma_start(wk[:], wk_in).then_inc(wqk_in_s, 16)
            for g in range(1, NG):
                sp.dma_start(x[:, g * GT:(g + 1) * GT, :], x_tiles[g]).then_inc(x_in_s[g], 16)
            sp.dma_start(w1, w1_in.rearrange("(m p) d -> p m d", p=P)).then_inc(ffn_in_s, 16)
            sp.dma_start(w2, w2_in).then_inc(ffn_in_s, 16)
            sp.dma_start(wr[:], wr_in).then_inc(ffn_in_s, 16)
            br_row = br_in.rearrange("(o n) -> o n", o=1)
            for i in range(GT):
                sp.dma_start(br[:, i, :], br_row.broadcast_to([P, NBLK])).then_inc(ffn_in_s, 16)
            for g in range(NG):
                sp.wait_ge(res_ready, g + 1)
                sp.dma_start(out_tiles[g], res[:, g % 2, :].rearrange("p (i d) -> p i d", i=GT)).then_inc(stored[g], 16)
            for g in range(NG):
                sp.wait_ge(stored[g], 16)

        @block.gpsimd
        def _(pool):
            steps = [0]

            def step(ins):
                steps[0] += 1
                ins.then_inc(pool_step, 1)
                pool.wait_ge(pool_step, steps[0])

            b1_row = b1_in.rearrange("(o n) -> o n", o=1)
            for r in (32, 64, 96):
                pool.dma_start(b1[r:r + 1, :], b1_row).then_inc(b1_in_s, 16)
            pool.memset(ident[:], 0.0)
            step(pool.memset(pow_half[:], -0.5))
            step(pool.affine_select(out=ident[:], in_=ident[:], compare_op=ALU.not_equal, fill=1.0, base=0,
                                    pattern=[[-1, P]], channel_multiplier=1))
            pool.tensor_copy(ident_b[:], ident[:]).then_inc(consts_made, 1)

            def norm(k, g):
                n, s = k * NG + g, slice(g * GT, (g + 1) * GT)
                src = x if k == 0 else x1
                pool.wait_ge(stats, n + 1)
                pool.tensor_scalar(nmean[:, k, s], mv[:, k, s, 0], -1.0, 0.0, ALU.mult, ALU.add)
                step(pool.tensor_scalar(rstd[:, k, s], mv[:, k, s, 1], EPS, 1.0, ALU.add, ALU.mult))
                step(pool.tensor_tensor(rstd[:, k, s], rstd[:, k, s], pow_half[:], ALU.pow))
                if n >= NG + 2:
                    pool.wait_ge(g_turned, n - NG - 1)
                elif n >= 2:
                    pool.wait_ge(xt_mm, n - 1)
                for i in range(GT):
                    t = g * GT + i
                    last = pool.tensor_scalar(xn[:, n % 2, i, :], src[:, t, :], nmean[:, k, t:t + 1],
                                              rstd[:, k, t:t + 1], ALU.add, ALU.mult)
                last.then_inc(xn_ready, 1)

            def low(full, hi, lo, full_s, hi_s, lo_s, n):
                pool.wait_ge(full_s, n)
                pool.wait_ge(hi_s, n)
                pool.tensor_tensor(lo, full, hi.bitcast(F32), ALU.subtract).then_inc(lo_s, 1)

            norm(0, 0)
            pool.wait_ge(wqk_in_s, 32)
            for w, hi, lo in ((wq, wq_hi, wq_lo), (wk, wk_hi, wk_lo)):
                step(pool.tensor_copy(hi[:], w[:]))
                pool.tensor_tensor(lo[:], w[:], hi[:].bitcast(F32), ALU.subtract).then_inc(qk_w_ready, 1)

            def project_lows(g):
                b = g % 2
                if g >= 2:
                    pool.wait_ge(v_mm, g - 1)
                low(h_full[:, b, :], h_hi[:, b, :], h_lo[:, b, :], h_full_s, h_hi_s, h_lo_s, g + 1)
                low(q_full[:, b, :], grp(q_hi, g), grp(q_lo, g), q_full_s, q_hi_s, q_lo_s, g + 1)
                low(k_full[:, b, :], grp(k_hi, g), grp(k_lo, g), k_full_s, k_hi_s, k_lo_s, g + 1)
                low(v_full[:, b, :], grp(v_hi, g), grp(v_lo, g), v_full_s, v_hi_s, v_lo_s, g + 1)

            step(pool.memset(causal[:], 0.0))
            pool.affine_select(out=causal[:], in_=causal[:], compare_op=ALU.is_ge, fill=FAR, base=0,
                               pattern=[[-1, P]], channel_multiplier=1).then_inc(consts_made, 1)
            norm(0, 1)
            pool.wait_ge(u_ready, 1)
            step(pool.tensor_copy(u_hi[:], u_full[:]))
            pool.tensor_tensor(u_lo[:], u_full[:], u_hi[:].bitcast(F32), ALU.subtract).then_inc(u_ready, 1)
            project_lows(0)
            norm(0, 2)
            project_lows(1)
            norm(0, 3)
            project_lows(2)
            project_lows(3)
            pool.wait_ge(gbo_ready, 1)
            for t in range(NT):
                last = pool.tensor_tensor(x[:, t, :], x[:, t, :], gbo_row[:], ALU.add)
            last.then_inc(xb_ready, 1)

            def key_low(t):
                if not pool_splits(t):
                    return
                s, w = t % 3, pt_cols[t]
                pool.wait_ge(pt_hi_dve, splits_before(t, True) + 1)
                if t >= 3:
                    pool.wait_ge(pv_done, t - 2)
                pool.tensor_tensor(pt_lo[:, s, w:], pt_full[:, splits_before(t, True) % 2, w:], pt_hi[:, s, w:].bitcast(F32),
                                   ALU.subtract).then_inc(pt_lo_pool, 1)

            def second_norm_low(g):
                if g >= 2:
                    pool.wait_ge(hid_mm, NH * (g - 1))
                else:
                    pool.wait_ge(v_mm, NG)
                low(g_full[:, g % 2, :], g_hi[:, g % 2, :], g_lo[:, g % 2, :], g_full_s, g_hi_s, g_lo_s, g + 1)

            def ffn_parts():
                pool.wait_ge(w_t_full, 2)
                for full, hi, lo in ((w1t_full, w1t_hi, w1t_lo), (w2t_full, w2t_hi, w2t_lo)):
                    step(pool.tensor_copy(hi[:], full[:]))
                    pool.tensor_tensor(lo[:], full[:], hi[:].bitcast(F32), ALU.subtract).then_inc(ffn_w_ready, 1)
                step(pool.memset(pick_f, 1.0))
                step(pool.affine_select(out=pick_f, in_=pick_f, compare_op=ALU.is_ge, fill=0.0, base=0,
                                        pattern=[[1, HID]], channel_multiplier=-BLK))
                step(pool.affine_select(out=pick_f, in_=pick_f, compare_op=ALU.is_ge, fill=0.0, base=BLK - 1,
                                        pattern=[[-1, HID]], channel_multiplier=BLK))
                step(pool.tensor_copy(pick[:], pick_f))
                pool.wait_ge(b1_in_s, 48)
                for k, r in enumerate((32, 64, 96)):
                    a = slice(r, r + 1)
                    for _ in range(k):
                        step(pool.tensor_copy(b1_part[a, :], b1[a, :]))
                        step(pool.tensor_tensor(b1[a, :], b1[a, :], b1_part[a, :], ALU.subtract))
                    step(pool.tensor_copy(pick[a, :], b1[a, :]))
                step(pool.memset(route[:], 0.0))
                for r in (32, 64, 96):
                    step(pool.memset(route[r:r + 1, :], 1.0))
                pool.memset(keys[:], 1.0).then_inc(pick_ready, 1)

            for g in range(NG):
                for what, a in mix(g):
                    if what == "key":
                        key_low(key_no(g, a))
                    elif what == "normalise":
                        norm(1, a)
                    elif what == "route":
                        second_norm_low(a)
                if g == 0:
                    ffn_parts()
            norm(1, NG - 1)
            second_norm_low(NG - 1)

        @block.scalar
        def _(act):
            act.dma_start(cols[:, C:C + 1], c_in.rearrange("o p -> p o")).then_inc(cols_in_s, 16)
            act.dma_start(wmod, wmod_in).then_inc(mod_in_s, 16)
            act.dma_start(wv[:], wv_in).then_inc(wvo_in_s, 16)
            act.dma_start(wo[:], wo_in).then_inc(wvo_in_s, 16)
            for n, v in ((BQ, bq_in), (BK, bk_in), (BV, bv_in), (BO, bo_in), (B2, b2_in)):
                act.dma_start(cols[:, n:n + 1], col(v)).then_inc(cols_in_s, 16)
            act.wait_ge(cols_in_s, 96)
            nc.scalar.activation(silu[:, 0:1], cols[:, C:C + 1], ACT.Exp, scale=-1.0).then_inc(silu_e, 1)
            act.wait_ge(wv_turned, 1)
            nc.scalar.copy(wv_t[:], score_bank[1][:, 0:P]).then_inc(wv_t_ready, 1)

            def project(g):
                b = g % 2
                act.wait_ge(xt_mm, g + 1)
                if g == 0:
                    act.wait_ge(mod_ready, 1)
                if g >= 2:
                    act.wait_ge(h_lo_s, g - 1)
                nc.scalar.activation(h_full[:, b, :], misc_bank[:], ACT.Identity, bias=mod[:, SA:SA + 1],
                                     scale=gate[:, CA:CA + 1]).then_inc(h_full_s, 1)
                act.wait_ge(q_mm, g + 1)
                if g >= 2:
                    act.wait_ge(q_lo_s, g - 1)
                nc.scalar.activation(q_full[:, b, :], turn_bank[0][:], ACT.Identity, bias=bqs[:],
                                     scale=QSCALE).then_inc(q_full_s, 1)
                act.wait_ge(k_mm, g + 1)
                if g >= 2:
                    act.wait_ge(k_lo_s, g - 1)
                nc.scalar.activation(k_full[:, b, :], turn_bank[1][:], ACT.Identity,
                                     bias=cols[:, BK:BK + 1]).then_inc(k_full_s, 1)

            def exps(g, r, c):
                n, w = g * GT + r, chunk_width(g, r, c)
                if c == 0:
                    act.wait_ge(nmax_ready, n + 1)
                    if r == 0 and g == 1:
                        act.wait_ge(w_turned, 2)
                    if r == 0 and g >= 2:
                        act.wait_ge(turned, key_no(g - 1, 0))
                nc.scalar.activation(probs[g % 2][:, r, c * GW:c * GW + w],
                                     score_bank[chunk_no(g, r, c) % 4][:, 0:w], ACT.Exp, bias=nmax[:, n:n + 1],
                                     accum_out=dpart[:, n, c:c + 1]).then_inc(exp_done, 1)

            def key_out(t):
                s, w = t % 3, pt_cols[t]
                act.wait_ge(turned, t + 1)
                if pool_splits(t):
                    n = splits_before(t, True)
                    if n >= 2:
                        act.wait_ge(pt_lo_pool, n - 1)
                    nc.scalar.copy(pt_full[:, n % 2, w:], turn_bank[t % 2][:, w:]).then_inc(pt_full_s, 1)
                else:
                    if t >= 3:
                        act.wait_ge(pv_done, t - 2)
                    nc.scalar.copy(pt_hi[:, s, w:], turn_bank[t % 2][:, w:]).then_inc(pt_hi_act, 1)

            def ctx_copy(g):
                act.wait_ge(pv_done, key_no(g + 1, 0))
                if g >= 1:
                    act.wait_ge(ctx_turned, g)
                else:
                    act.wait_ge(q_lo_s, NG)
                nc.scalar.activation(ctx_sb, ctx_bank[:], ACT.Identity, scale=gate[:, GA:GA + 1]).then_inc(ctx_out, 1)

            def second_norm(g):
                act.wait_ge(g_turned, g + 1)
                if g >= 2:
                    act.wait_ge(hid_mm, NH * (g - 1))
                    act.wait_ge(g_lo_s, g - 1)
                    act.wait_ge(logits_mm, g - 1)
                else:
                    act.wait_ge(h_lo_s, NG)
                nc.scalar.activation(g_full[:, g % 2, :], misc_bank[:], ACT.Identity, bias=mod[:, SB_:SB_ + 1],
                                     scale=gate[:, CB:CB + 1]).then_inc(g_full_s, 1)

            def route_copy(g):
                act.wait_ge(nmask_turned, g + 1)
                act.wait_ge(pick_ready, 1)
                nc.scalar.copy(route[0:NBLK, g * GW:(g + 1) * GW],
                               misc_bank[0:NBLK, 0:GW // 2].bitcast(BF16)).then_inc(route_ready, 1)

            def hidden(g, m):
                act.wait_ge(hid_mm, g * NH + m + 1)
                if g >= 1:
                    act.wait_ge(y_mm, (g - 1) * NH + m + 1)
                nc.scalar.activation(hid_hi[:, m, :], score_bank[(CHUNKS + g * NH + m) % 4][:], ACT.Relu).then_inc(hid_hi_s, 1)

            def y_copy(g):
                act.wait_ge(y_mm, NH * (g + 1))
                if g >= 1:
                    act.wait_ge(y_turned, g)
                else:
                    act.wait_ge(k_lo_s, NG)
                nc.scalar.activation(y_sb, turn_bank[g % 2][:], ACT.Identity, bias=gbb2[:],
                                     scale=gate[:, GB:GB + 1]).then_inc(y_out, 1)

            project(0)
            project(1)
            project(2)
            for r in range(GT):
                exps(0, r, 0)
            project(3)
            for g in range(NG):
                queue = [(g + 1, r, c) for r in range(GT) for c in range(g + 2)] if g + 1 < NG else []
                seen = 0
                for what, a in mix(g):
                    if what == "score":
                        seen += 1
                        if seen > g + 2:
                            exps(*queue.pop(0))
                    elif what == "key":
                        key_out(key_no(g, a))
                    elif what == "turn norm":
                        second_norm(a)
                    elif what == "mask":
                        route_copy(a)
                    elif what == "hidden":
                        hidden(0, a)
                for q in queue:
                    exps(*q)
                ctx_copy(g)
            y_copy(0)
            for g in range(1, NG):
                for m in range(NH):
                    hidden(g, m)
                if g == 1:
                    second_norm(NG - 1)
                y_copy(g)
                if g == 1:
                    route_copy(NG - 1)

        @block.vector
        def _(dve):
            steps = [0]

            def step(ins):
                steps[0] += 1
                ins.then_inc(dve_step, 1)
                dve.wait_ge(dve_step, steps[0])

            def norm_stats(k, g):
                src = x if k == 0 else x1
                if k == 0:
                    dve.wait_ge(x_in_s[g], 16)
                for i in range(GT):
                    last = nc.vector.bn_stats(st[:, k, g * GT + i, :], src[:, g * GT + i, :])
                step(last)
                for i in range(GT):
                    last = nc.vector.bn_aggr(mv[:, k, g * GT + i, :], st[:, k, g * GT + i, :])
                last.then_inc(stats, 1)

            norm_stats(0, 0)
            dve.wait_ge(silu_e, 1)
            step(nc.vector.tensor_scalar(silu[:, 1:2], silu[:, 0:1], 1.0, None, ALU.add))
            step(nc.vector.reciprocal(silu[:, 2:3], silu[:, 1:2]))
            nc.vector.tensor_tensor(silu[:, 3:4], silu[:, 2:3], cols[:, C:C + 1], ALU.mult).then_inc(silu_e, 1)
            dve.wait_ge(cols_in_s, 96)
            nc.vector.tensor_scalar(bqs[:], cols[:, BQ:BQ + 1], QSCALE, None, ALU.mult)
            dve.wait_ge(consts_made, 1)
            nc.vector.tensor_scalar(bv_wide[:], ident[:], 0.0, cols[:, BV:BV + 1], ALU.mult, ALU.add).then_inc(wide_ready, 1)
            norm_stats(0, 1)
            dve.wait_ge(mod_mm, 1)
            step(nc.vector.tensor_copy(mod[:], score_bank[0][:, 0:6]))
            for s in (CA, CB):
                nc.vector.tensor_scalar(gate[:, s:s + 1], mod[:, s:s + 1], 1.0, None, ALU.add)
            for s, sign in ((GA, SA), (GB, SB_)):
                step(nc.vector.tensor_scalar(gate[:, sign:sign + 1], mod[:, s:s + 1], 0.0, 2.0, ALU.is_ge, ALU.mult))
                step(nc.vector.tensor_scalar(gate[:, sign:sign + 1], gate[:, sign:sign + 1], -1.0, None, ALU.add))
                step(nc.vector.tensor_scalar(gate[:, s:s + 1], mod[:, s:s + 1], gate[:, sign:sign + 1], 0.25,
                                             ALU.mult, ALU.max))
                step(nc.vector.tensor_scalar(gate[:, s:s + 1], gate[:, s:s + 1], gate[:, sign:sign + 1], None, ALU.mult))
            nc.vector.tensor_scalar(gbb2[:], gate[:, GB:GB + 1], cols[:, B2:B2 + 1], None, ALU.mult).then_inc(mod_ready, 1)
            nc.vector.tensor_scalar(gbo_wide[:, 0:1], gate[:, GA:GA + 1], cols[:, BO:BO + 1], None, ALU.mult).then_inc(wide_ready, 1)
            dve.wait_ge(wide_ready, 2)
            nc.vector.tensor_scalar(gbo_wide[:, 1:P], ident[:, 1:P], 0.0, gbo_wide[:, 0:1], ALU.mult, ALU.add).then_inc(wide_ready, 1)
            dve.wait_ge(u_mm, 1)
            nc.vector.tensor_copy(bv_out[:], score_bank[2][:, P:2 * P])
            nc.vector.tensor_copy(u_full[:], score_bank[2][:, 0:P]).then_inc(u_ready, 1)

            def high(hi, full, full_s, hi_s, n):
                dve.wait_ge(full_s, n)
                nc.vector.tensor_copy(hi, full).then_inc(hi_s, 1)

            def project(g):
                b = g % 2
                if g >= 2:
                    dve.wait_ge(v_mm, g - 1)
                high(h_hi[:, b, :], h_full[:, b, :], h_full_s, h_hi_s, g + 1)
                high(grp(q_hi, g), q_full[:, b, :], q_full_s, q_hi_s, g + 1)
                high(grp(k_hi, g), k_full[:, b, :], k_full_s, k_hi_s, g + 1)
                dve.wait_ge(v_mm, g + 1)
                if g >= 2:
                    dve.wait_ge(v_lo_s, g - 1)
                nc.vector.tensor_tensor(v_full[:, b, :].rearrange("p (i d) -> p i d", i=GT),
                                        ctx_bank[:].rearrange("p (i d) -> p i d", i=GT),
                                        bv_out[:].rearrange("p (o d) -> p o d", o=1).broadcast_to([P, GT, P]),
                                        ALU.add).then_inc(v_full_s, 1)
                high(grp(v_hi, g), v_full[:, b, :], v_full_s, v_hi_s, g + 1)

            def row_max(g, r, c):
                n, w, k = g * GT + r, chunk_width(g, r, c), chunk_no(g, r, c)
                dve.wait_ge(scored, k + 1)
                if g == 0:
                    nc.vector.tensor_reduce(nmax[:, n:n + 1], score_bank[k % 4][:, 0:w], AX.X, ALU.max,
                                            negate=True).then_inc(nmax_ready, 1)
                    return
                last = nc.vector.tensor_reduce(cmax[:, n, c:c + 1], score_bank[k % 4][:, 0:w], AX.X, ALU.max)
                if c == g:
                    step(last)
                    nc.vector.tensor_reduce(nmax[:, n:n + 1], cmax[:, n, 0:g + 1], AX.X, ALU.max,
                                            negate=True).then_inc(nmax_ready, 1)

            def key_split(t):
                s, w = t % 3, pt_cols[t]
                if pool_splits(t):
                    dve.wait_ge(pt_full_s, splits_before(t, True) + 1)
                    if t >= 3:
                        dve.wait_ge(pv_done, t - 2)
                    nc.vector.tensor_copy(pt_hi[:, s, w:], pt_full[:, splits_before(t, True) % 2, w:]).then_inc(pt_hi_dve, 1)
                else:
                    dve.wait_ge(pt_hi_act, splits_before(t, False) + 1)
                    if t >= 3:
                        dve.wait_ge(pv_done, t - 2)
                    nc.vector.tensor_tensor(pt_lo[:, s, w:], turn_bank[t % 2][:, w:], pt_hi[:, s, w:].bitcast(F32),
                                            ALU.subtract).then_inc(pt_lo_dve, 1)

            def attention_out(g):
                s = slice(g * GT, (g + 1) * GT)
                dve.wait_ge(exp_done, chunk_no(g + 1, 0, 0))
                step(nc.vector.tensor_reduce(den[:, s], dpart[:, s, 0:g + 1], AX.X, ALU.add))
                step(nc.vector.reciprocal(rden[:, s], den[:, s]))
                dve.wait_ge(ctx_turned, g + 1)
                if g == 0:
                    dve.wait_ge(xb_ready, 1)
                for i in range(GT):
                    t = g * GT + i
                    last = nc.vector.scalar_tensor_tensor(out=x1[:, t, :], in0=tile(misc_bank, i),
                                                          scalar=rden[:, t:t + 1], in1=x[:, t, :],
                                                          op0=ALU.mult, op1=ALU.add)
                last.then_inc(x1_ready, 1)
                dve.wait_ge(x1_ready, g + 1)
                norm_stats(1, g)

            def second_norm(g):
                if g >= 2:
                    dve.wait_ge(hid_mm, NH * (g - 1))
                else:
                    dve.wait_ge(v_mm, NG)
                high(g_hi[:, g % 2, :], g_full[:, g % 2, :], g_full_s, g_hi_s, g + 1)

            def choose(g):
                dve.wait_ge(logits_mm, g + 1)
                if g == 0:
                    dve.wait_ge(pick_ready, 1)
                step(nc.vector.tensor_tensor(logit[:], misc_bank[:, 0:GT * NBLK].rearrange("p (i e) -> p i e", i=GT),
                                             br[:], ALU.add))
                step(nc.vector.tensor_reduce(lmax[:], logit[:], AX.X, ALU.max))
                step(nc.vector.tensor_tensor(ldiff[:], logit[:],
                                             lmax[:].rearrange("p (i o) -> p i o", o=1).broadcast_to([P, GT, NBLK]),
                                             ALU.subtract))
                step(nc.vector.tensor_scalar(keys[:, :, 0:NBLK], ldiff[:], UNDER, None, ALU.max))
                for i in range(GT):
                    last = nc.vector.max(top8[:, i, :], keys[:, i, :])
                step(last)
                for i in range(GT):
                    last = nc.vector.match_replace(marked[:, i, :], top8[:, i, :], keys[:, i, :], 1.0)
                step(last)
                if g >= 1:
                    dve.wait_ge(nmask_turned, g)
                nc.vector.tensor_scalar(nmask[:], marked[:, :, 0:NBLK], 0.0, FAR, ALU.is_le, ALU.mult).then_inc(nmask_ready, 1)

            def hidden(g, m):
                n = g * NH + m
                dve.wait_ge(hid_hi_s, n + 1)
                if g >= 1:
                    dve.wait_ge(y_mm, (g - 1) * NH + m + 1)
                nc.vector.scalar_tensor_tensor(out=hid_lo[:, m, :], in0=score_bank[(CHUNKS + n) % 4][:], scalar=0.0,
                                               in1=hid_hi[:, m, :].bitcast(F32), op0=ALU.max,
                                               op1=ALU.subtract).then_inc(hid_lo_s, 1)

            def finish(g):
                dve.wait_ge(y_turned, g + 1)
                if g >= 2:
                    dve.wait_ge(stored[g - 2], 16)
                elif g == 0:
                    dve.wait_ge(v_lo_s, NG)
                nc.vector.tensor_tensor(res[:, g % 2, :], ctx_bank[:],
                                        x1[:, g * GT:(g + 1) * GT, :].rearrange("p i d -> p (i d)"),
                                        ALU.add).then_inc(res_ready, 1)

            def ffn_weights():
                dve.wait_ge(w_turned, 1)
                nc.vector.tensor_copy(w1t_full[:], score_bank[0][:]).then_inc(w_t_full, 1)
                dve.wait_ge(w_turned, 2)
                nc.vector.tensor_copy(w2t_full[:], score_bank[1][:]).then_inc(w_t_full, 1)

            norm_stats(0, 2)
            project(0)
            dve.wait_ge(gbo_mm, 1)
            nc.vector.tensor_copy(gbo_row[:], score_bank[3][:, 0:P]).then_inc(gbo_ready, 1)
            norm_stats(0, 3)
            ffn_weights()
            project(1)
            for r in range(GT):
                row_max(0, r, 0)
            project(2)
            project(3)
            for g in range(NG):
                for what, a in mix(g):
                    if what == "score":
                        row_max(g + 1, *a)
                    elif what == "key":
                        key_split(key_no(g, a))
                    elif what == "route":
                        second_norm(a)
                        choose(a)
                    elif what == "hidden":
                        hidden(0, a)
                attention_out(g)
            for g in range(1, NG):
                for m in range(NH):
                    hidden(g, m)
                if g == 1:
                    second_norm(NG - 1)
                    choose(NG - 1)
                finish(g - 1)
            finish(NG - 1)

        @block.tensor
        def _(pe):
            mm = nc.tensor.matmul

            def three(dst, w_hi, w_lo, m_hi, m_lo, hi_wait, lo_wait, start=True, stop=True):
                if hi_wait:
                    pe.wait_ge(*hi_wait)
                mm(dst, w_hi, m_hi, start=start, stop=False)
                mm(dst, w_lo, m_hi, start=False, stop=False)
                if lo_wait:
                    pe.wait_ge(*lo_wait)
                return mm(dst, w_hi, m_lo, start=False, stop=stop)

            pe.wait_ge(consts_made, 1)
            pe.wait_ge(wvo_in_s, 32)
            nc.tensor.transpose(score_bank[1][:, 0:P], wv[:], ident[:]).then_inc(wv_turned, 1)

            def turn_norm(n):
                pe.wait_ge(xn_ready, n + 1)
                for i in range(GT):
                    last = nc.tensor.transpose(tile(misc_bank, i), xn[:, n % 2, i, :], ident[:])
                last.then_inc(xt_mm, 1)
                return last

            def project(g):
                b = g % 2
                pe.wait_ge(qk_w_ready, 2)
                if g >= 1:
                    pe.wait_ge(q_full_s, g)
                three(turn_bank[0][:], wq_hi[:], wq_lo[:], h_hi[:, b, :], h_lo[:, b, :],
                      (h_hi_s, g + 1), (h_lo_s, g + 1)).then_inc(q_mm, 1)
                if g >= 1:
                    pe.wait_ge(k_full_s, g)
                three(turn_bank[1][:], wk_hi[:], wk_lo[:], h_hi[:, b, :], h_lo[:, b, :], None, None).then_inc(k_mm, 1)
                pe.wait_ge(u_ready, 2)
                if g >= 1:
                    pe.wait_ge(v_full_s, g)
                for i in range(GT):
                    last = three(tile(ctx_bank, i), h_hi[:, b, i * P:(i + 1) * P], h_lo[:, b, i * P:(i + 1) * P],
                                 u_hi[:], u_lo[:], None, None)
                last.then_inc(v_mm, 1)

            def score(g, r, c):
                k, w, t = chunk_no(g, r, c), chunk_width(g, r, c), g * GT + r
                if k >= 4:
                    pe.wait_ge(exp_done, k - 3)
                if c == 0 and r == 0:
                    pe.wait_ge(q_hi_s, g + 1)
                    pe.wait_ge(q_lo_s, g + 1)
                    pe.wait_ge(k_hi_s, g + 1)
                    pe.wait_ge(k_lo_s, g + 1)
                dst = score_bank[k % 4][:, 0:w]
                last = three(dst, tile(q_hi, t), tile(q_lo, t), k_hi[:, c * GW:c * GW + w],
                             k_lo[:, c * GW:c * GW + w], None, None, stop=(c < g))
                if c == g:
                    last = mm(score_bank[k % 4][:, w - P:w], ident_b[:], causal[:], start=False, stop=True)
                last.then_inc(scored, 1)

            def turn_keys(g, j):
                t = key_no(g, j)
                pe.wait_ge(exp_done, chunk_no(g, GT - 1, j // GT) + 1)
                if t < 2:
                    pe.wait_ge((q_full_s, k_full_s)[t], NG)
                else:
                    p = t - 2
                    if pool_splits(p):
                        pe.wait_ge(pt_full_s, splits_before(p, True) + 1)
                    else:
                        pe.wait_ge(pt_lo_dve, splits_before(p, False) + 1)
                for r in range(key_from(g, j), GT):
                    last = nc.tensor.transpose(turn_bank[t % 2][:, r * P:(r + 1) * P],
                                               probs[g % 2][:, r, j * P:(j + 1) * P], ident[:])
                last.then_inc(turned, 1)

            def weigh(g, j):
                t, last_j = key_no(g, j), GT * (g + 1) - 1
                s, w = t % 3, pt_cols[t]
                if pool_splits(t):
                    hi, lo = (pt_hi_dve, splits_before(t, True) + 1), (pt_lo_pool, splits_before(t, True) + 1)
                else:
                    hi, lo = (pt_hi_act, splits_before(t, False) + 1), (pt_lo_dve, splits_before(t, False) + 1)
                if j == 0:
                    if g == 0:
                        pe.wait_ge(v_full_s, NG)
                    else:
                        pe.wait_ge(ctx_out, g)
                    pe.wait_ge(v_hi_s, g + 1)
                    pe.wait_ge(v_lo_s, g + 1)
                three(ctx_bank[:, w:], tile(v_hi, j), tile(v_lo, j), pt_hi[:, s, w:], pt_lo[:, s, w:],
                      hi, lo, start=(j == 0), stop=(j == last_j)).then_inc(pv_done, 1)

            def turn_context(g):
                pe.wait_ge(ctx_out, g + 1)
                if g == 0:
                    pe.wait_ge(h_full_s, NG)
                else:
                    pe.wait_ge(route_ready, g)
                for i in range(GT):
                    last = nc.tensor.transpose(tile(misc_bank, i), ctx_sb[:, i * P:(i + 1) * P], ident[:])
                last.then_inc(ctx_turned, 1)

            def turn_second_norm(g):
                pe.wait_ge(x1_ready, g + 1)
                pe.wait_ge(xn_ready, NG + g + 1)
                for i in range(GT):
                    last = nc.tensor.transpose(tile(misc_bank, i), xn[:, (NG + g) % 2, i, :], ident[:])
                last.then_inc(g_turned, 1)

            def router(g):
                pe.wait_ge(g_full_s, g + 1)
                if g == 0:
                    pe.wait_ge(ffn_in_s, 16 * (3 + GT))
                for i in range(GT):
                    last = mm(misc_bank[:, i * NBLK:(i + 1) * NBLK], g_full[:, g % 2, i * P:(i + 1) * P], wr[:],
                              start=True, stop=True)
                last.then_inc(logits_mm, 1)

            def turn_mask(g):
                pe.wait_ge(nmask_ready, g + 1)
                for i in range(GT):
                    last = nc.tensor.transpose(misc_bank[0:NBLK, i * P // 2:(i + 1) * P // 2].bitcast(BF16),
                                               nmask[:, i, :], ident_b[:])
                last.then_inc(nmask_turned, 1)

            def hidden(g, m):
                n = g * NH + m
                if n < 4:
                    pe.wait_ge(exp_done, CHUNKS - 3 + n)
                else:
                    pe.wait_ge(hid_lo_s, n - 3)
                if m == 0:
                    pe.wait_ge(route_ready, g + 1)
                    pe.wait_ge(ffn_w_ready, 2)
                dst = score_bank[(CHUNKS + n) % 4][:]
                three(dst, tile(w1t_hi, m), tile(w1t_lo, m), g_hi[:, g % 2, :], g_lo[:, g % 2, :],
                      (g_hi_s, g + 1), (g_lo_s, g + 1), stop=False)
                mm(dst, tile(pick, m), grp(route, g), start=False, stop=True).then_inc(hid_mm, 1)

            def down(g, m):
                n = g * NH + m
                if m == 0:
                    if g < 2:
                        pe.wait_ge(pt_lo_dve, splits_before(len(pt_cols), False))
                        pe.wait_ge(pt_full_s, splits_before(len(pt_cols), True))
                    else:
                        pe.wait_ge(y_out, g - 1)
                three(turn_bank[g % 2][:], tile(w2t_hi, m), tile(w2t_lo, m), hid_hi[:, m, :], hid_lo[:, m, :],
                      (hid_hi_s, n + 1), (hid_lo_s, n + 1), start=(m == 0), stop=(m == NH - 1)).then_inc(y_mm, 1)

            def turn_y(g):
                pe.wait_ge(y_out, g + 1)
                if g >= 1:
                    pe.wait_ge(res_ready, g)
                for i in range(GT):
                    last = nc.tensor.transpose(tile(ctx_bank, i), y_sb[:, i * P:(i + 1) * P], ident[:])
                last.then_inc(y_turned, 1)

            turn_norm(0)
            pe.wait_ge(silu_e, 2)
            pe.wait_ge(mod_in_s, 16)
            for n in range(6):
                last = mm(score_bank[0][:, n:n + 1], tile(wmod, n), silu[:, 3:4], start=True, stop=True)
            last.then_inc(mod_mm, 1)
            pe.wait_ge(wv_t_ready, 1)
            pe.wait_ge(wide_ready, 1)
            mm(score_bank[2][:, 0:P], wv_t[:], wo[:], start=True, stop=True)
            mm(score_bank[2][:, P:2 * P], bv_wide[:], wo[:], start=True, stop=True).then_inc(u_mm, 1)
            pe.wait_ge(wide_ready, 3)
            mm(score_bank[3][:, 0:P], gbo_wide[:], ident[:], start=True, stop=True).then_inc(gbo_mm, 1)
            project(0)
            pe.wait_ge(h_full_s, 1)
            turn_norm(1)
            pe.wait_ge(ffn_in_s, 16 * (3 + GT))
            pe.wait_ge(mod_ready, 1)
            for m in range(NH):
                last = nc.tensor.transpose(tile(score_bank[0], m), w1[:, m, :], ident[:])
            last.then_inc(w_turned, 1)
            for m in range(NH):
                last = nc.tensor.transpose(tile(score_bank[1], m), tile(w2, m), ident[:])
            last.then_inc(w_turned, 1)
            project(1)
            pe.wait_ge(h_full_s, 2)
            turn_norm(2)
            pe.wait_ge(w_t_full, 2)
            pe.wait_ge(gbo_ready, 1)
            pe.wait_ge(consts_made, 2)
            for r in range(GT):
                score(0, r, 0)
            project(2)
            pe.wait_ge(h_full_s, 3)
            turn_norm(3)
            project(3)
            for g in range(NG):
                ahead = []
                for what, a in mix(g):
                    if what == "score":
                        score(g + 1, *a)
                    elif what == "key":
                        turn_keys(g, a)
                        ahead.append(a)
                        if len(ahead) > 2:
                            weigh(g, ahead.pop(0))
                    elif what == "turn norm":
                        turn_second_norm(a)
                    elif what == "route":
                        router(a)
                    elif what == "mask":
                        turn_mask(a)
                    elif what == "hidden":
                        hidden(0, a)
                for a in ahead:
                    weigh(g, a)
                turn_context(g)
            for m in range(NH):
                down(0, m)
            for g in range(1, NG):
                for m in range(NH):
                    hidden(g, m)
                turn_y(g - 1)
                if g == 1:
                    turn_second_norm(NG - 1)
                    router(NG - 1)
                for m in range(NH):
                    down(g, m)
                if g == 1:
                    turn_mask(NG - 1)
            turn_y(NG - 1)


_INS = ['L0_attn_y_all', 'L0_attn_Wq', 'L0_attn_bq', 'L0_attn_Wk', 'L0_attn_bk', 'L0_attn_Wv', 'L0_attn_bv',
        'L0_attn_Wo', 'L0_attn_bo', 'L0_ffn_w_router', 'L0_ffn_b_router', 'L0_ffn_w1', 'L0_ffn_b1', 'L0_ffn_w2',
        'L0_ffn_b2', 'L0_c', 'L0_wmod']
_OUTS = [((1, 2048, 128), 'float32')]


def kernel(**inputs):
    import numpy as _np
    import concourse.bacc as _bacc
    from concourse import mybir as _mybir
    from concourse.bass_utils import run_bass_kernel_spmd as _run

    nc = _bacc.Bacc("TRN2", target_bir_lowering=False, num_devices=1)
    arrays, args = {}, []
    for name in _INS:
        a = _np.ascontiguousarray(inputs[name])
        arrays[f"in_{name}_dram"] = a
        args.append(nc.dram_tensor(f"in_{name}_dram", a.shape, _mybir.dt.from_np(a.dtype), kind="ExternalInput").ap())
    for i, (shape, dtype) in enumerate(_OUTS):
        dt = _mybir.dt.from_np(_np.dtype(dtype))
        args.append(nc.dram_tensor(f"out_{i}_dram", shape, dt, kind="ExternalOutput").ap())
    adaln_attention_sparse_ffn(nc, *args)
    r = _run(nc, [arrays], core_ids=[0])
    got = tuple(r.results[0][f"out_{i}_dram"] for i in range(len(_OUTS)))
    return got[0]
```

```python
from contextlib import ExitStack

import concourse.bass as bass
from concourse import mybir

ALU = mybir.AluOpType
ACT = mybir.ActivationFunctionType
AX = mybir.AxisListType
F32 = mybir.dt.float32
F32R = mybir.dt.float32r
BF16 = mybir.dt.bfloat16


P = 128
GT = 4
GW = GT * P
EPS = 1e-5
FAR = -1e30
RING = 6
UNDER = -87.33

TENSOR_PLAN = """
s0 s1 s2 s3 s4 n3 s5 q2 s6 k2 s7 v2 s8 q3 s9 k3 s10 v3 s11 t0 s12 t1 s13 t2 t3 s14 w0 s15 w1 t4 s16 s17 t5 s18
w2 t6 w3 t7 s19 c0 t8 s20 s21 w4 t9 w5 w6 w7 s22 t10 s23 s24 t11 n4 w8 w9 w10 w11 s25 t12 s26 s27 t13 r0 t14
t15 w12 s28 s29 s30 s31 w13 m0 t16 t17 w14 c1 w15 s32 t18 s33 t19 s34 s35 w16 t20 t21 w17 n5 w18 t22 t23 w19
w20 s36 s37 w21 s38 s39 w22 w23 r1 t24 t25 h0 h1 m1 h2 t26 t27 w24 w25 c2 t28 t29 w26 w27 h3 h4 t30 t31 w28
w29 n6 t32 t33 w30 w31 t34 t35 w32 w33 t36 t37 w34 r2 t38 t39 w35 w36 w37 h5 m2 w38 w39 d0 h6 c3 h7 h8 d1 d2
d3 d4 d5 h9 n7 h10 h11 d6 d7 r3 d8 d9 d10 y0 d11 m3 y1 h12 h13 h14 h15 d12 d13 d14 d15 y2 y3
"""
SCALAR_PLAN = """
n2 e0 e1 e2 n3 e3 q2 e4 k2 e5 v2 e6 q3 e7 k3 e8 e9 v3 t0 t1 e10 e11 t2 t3 e12 e13 e14 t4 t5 e15 t6 c0 e16 e17
t7 t8 t9 e18 e19 e20 t10 t11 n4 e21 e22 e23 c1 t12 t13 e24 e25 e26 e27 t14 t15 m0 t16 e28 t17 e29 e30 t18 e31
t19 t20 t21 n5 t22 e32 e33 e34 e35 t23 c2 e36 e37 e38 t24 t25 e39 m1 h0 t26 t27 h1 h2 t28 t29 h3 t30 t31 n6
t32 t33 t34 t35 t36 t37 t38 t39 m2 c3 h4 h5 h6 h7 y0 h8 h9 n7 h10 h11 y1 m3 y2 h12 h13 h14 h15 y3
"""
VECTOR_PLAN = """
a3 s0 n2 s1 s2 s3 s4 n3 s5 s6 q2 s7 k2 s8 v2 s9 q3 s10 k3 s11 t0 s12 v3 s13 s14 t2 s15 s16 t4 s17 s18 t6 s19
x0 s20 t8 s21 a4 s22 t10 s23 s24 n4 s25 s26 t12 s27 m0 s28 s29 t14 s30 s31 t16 x1 s32 t18 s33 a5 s34 t20 s35
n5 t22 s36 s37 s38 s39 m1 t24 h0 t26 x2 t28 h1 h2 a6 t30 h3 n6 t32 t34 t36 m2 t38 h4 x3 h5 h6 a7 h7 h8 h9 n7
h10 h11 m3 f0 f1 h12 h13 h14 h15 f2 f3
"""
GPSIMD_PLAN = """
t1 t3 t5 t7 p4 t9 t11 t13 t15 t17 p5 t19 t21 t23 t25 t27 t29 p6 t31 t33 t35 t37 t39 p7
"""


def adaln_attention_sparse_ffn(nc, x_in, wq_in, bq_in, wk_in, bk_in, wv_in, bv_in, wo_in, bo_in,
                               wr_in, br_in, w1_in, b1_in, w2_in, b2_in, c_in, wmod_in, out):
    _, T, D = x_in.shape
    HID = w1_in.shape[0]
    NBLK = wr_in.shape[1]
    TOPK = NBLK // 4
    BLK = HID // NBLK
    NT = T // P
    NG = T // GW
    NH = HID // P
    PADS = 8 - TOPK
    KEYS = NBLK + PADS
    QSCALE = float(D) ** -0.5
    assert D == P and wq_in.shape[1] == P and HID == GW and NG == 4

    def chunk_no(g, r, c):
        return sum(GT * (k + 1) for k in range(g)) + r * (g + 1) + c

    def chunk_width(g, r, c):
        return GW if c < g else P * (r + 1)

    def key_no(g, j):
        return sum(GT * (k + 1) for k in range(g)) + j

    def key_from(g, j):
        return max(0, j - GT * g)

    CHUNKS = chunk_no(NG, 0, 0)
    KEY_TILES = key_no(NG, 0)
    chunk_of = [(g, r, c) for g in range(NG) for r in range(GT) for c in range(g + 1)]
    key_of = [(g, j) for g in range(NG) for j in range(GT * (g + 1))]
    pt_cols = [P * key_from(g, j) for g in range(NG) for j in range(GT * (g + 1))]

    def pool_splits(t):
        return t % 2 == 1

    def splits_before(t, by_pool):
        return sum(pool_splits(k) == by_pool for k in range(t))

    def run(plan, steps):
        for word in plan.split():
            steps[word[0]](int(word[1:]))

    with ExitStack() as ctx:
        def sb(name, shape, dt=F32):
            return ctx.enter_context(nc.sbuf_tensor(name, shape, dt))

        def sem(name):
            return ctx.enter_context(nc.semaphore(name))

        bank = [ctx.enter_context(nc.psum_tensor(f"bank{i}", [P, GW], F32)) for i in range(8)]
        score_bank = bank[0:4]
        turn_bank = bank[4:6]
        ctx_bank, misc_bank = bank[6], bank[7]

        x = sb("x", [P, NT, D])
        x1 = x
        xn = sb("xn", [P, 2, GT, D])
        h_hi = sb("h_hi", [P, T], F32R)
        h_lo = sb("h_lo", [P, T], F32R)
        q_hi = sb("q_hi", [P, T], F32R)
        q_lo = sb("q_lo", [P, T], F32R)
        k_hi = sb("k_hi", [P, T], F32R)
        k_lo = sb("k_lo", [P, T], F32R)
        v_hi = sb("v_hi", [P, T], F32R)
        v_lo = sb("v_lo", [P, T], F32R)
        probs = [sb("probs0", [P, GT, 3 * GW]), sb("probs1", [P, GT, 4 * GW])]
        pt_full = sb("pt_full", [P, 2, GW])
        pt_hi = sb("pt_hi", [P, RING, GW], F32R)
        pt_lo = sb("pt_lo", [P, RING, GW], F32R)
        ctx_sb = sb("ctx_sb", [P, GW])
        hid_hi = q_hi[:].rearrange("p (m t) -> p m t", m=NH)
        hid_lo = q_lo[:].rearrange("p (m t) -> p m t", m=NH)
        y_sb = sb("y_sb", [P, GW])
        res = sb("res", [P, 2, GW])
        wq, wk, wv, wo = (sb(n, [P, P]) for n in ("wq", "wk", "wv", "wo"))
        wq_full, wk_full = sb("wq_full", [P, P]), sb("wk_full", [P, P])
        wq_hi, wk_hi, u_hi = (sb(n, [P, P], F32R) for n in ("wq_hi", "wk_hi", "u_hi"))
        wq_lo, wk_lo, u_lo = (sb(n, [P, P], F32R) for n in ("wq_lo", "wk_lo", "u_lo"))
        wv_t = sb("wv_t", [P, P])
        u_full = sb("u_full", [P, P])
        shift_wide = sb("shift_wide", [P, P])
        gbo_wide = sb("gbo_wide", [P, P])
        gbo_row = sb("gbo_row", [P, P])
        w1 = probs[1][:, 0, 0:HID].rearrange("p (m d) -> p m d", m=NH)
        w2 = probs[1][:, 1, 0:HID]
        wmod = probs[1][:, 2, 0:6 * D]
        w1t_full = sb("w1t_full", [P, HID])
        w1t_hi, w1t_lo = sb("w1t_hi", [P, HID], F32R), sb("w1t_lo", [P, HID], F32R)
        w2t_hi, w2t_lo = sb("w2t_hi", [P, HID], F32R), sb("w2t_lo", [P, HID], F32R)
        wr = sb("wr", [P, NBLK])
        wr_full = sb("wr_full", [P, NBLK])
        wr_hi, wr_lo = sb("wr_hi", [P, NBLK], F32R), sb("wr_lo", [P, NBLK], F32R)
        br = sb("br", [P, GT, NBLK])
        cols = sb("cols", [P, 6])
        BQ, BK, BV, BO, B2, C = range(6)
        silu = sb("silu", [P, 4])
        mod = sb("mod", [P, 6])
        SA, CA, GA, SB_, CB, GB = range(6)
        gate = sb("gate", [P, 6])
        qk_bias = sb("qk_bias", [P, 2])
        v_bias = sb("v_bias", [P, 2])
        gbb2 = sb("gbb2", [P, 1])
        ident = sb("ident", [P, P])
        ident_b = sb("ident_b", [P, P], BF16)
        causal = sb("causal", [P, P], BF16)
        pow_half = sb("pow_half", [P, GT])
        pick = sb("pick", [P, HID], BF16)
        route = sb("route", [P, T], BF16)
        b1 = sb("b1", [P, HID])
        b1_part = sb("b1_part", [P, HID], BF16)
        st = sb("st", [P, 2, NT, 6])
        mv = sb("mv", [P, 2, NT, 2])
        rstd = sb("rstd", [P, 2, NT])
        cmax = sb("cmax", [P, NT, NG])
        nmax = sb("nmax", [P, NT])
        dpart = sb("dpart", [P, NT, NG])
        den = sb("den", [P, NT])
        rden = sb("rden", [P, NT])
        logit = sb("logit", [P, GT, NBLK])
        lmax = sb("lmax", [P, GT])
        ldiff = sb("ldiff", [P, GT, NBLK])
        keys = sb("keys", [P, GT, KEYS])
        top8 = sb("top8", [P, GT, 8])
        marked = sb("marked", [P, GT, KEYS])
        nmask = sb("nmask", [P, GT, NBLK], BF16)

        x_in_s = [sem(f"x_loaded{g}") for g in range(NG)]
        mod_in_s, cols_in_s, wqk_in_s, wvo_in_s = (sem(n) for n in ("wmod_loaded", "cols_loaded", "wqk_loaded", "wvo_loaded"))
        ffn_in_s, b1_in_s = sem("ffn_weights_loaded"), sem("b1_loaded")
        c_in_s, b1_full_s, gate_ready = sem("c_loaded"), sem("b1_full_s"), sem("gate_ready")
        stored = [sem(f"stored{g}") for g in range(NG)]
        consts_made = sem("consts_made")
        silu_s, mod_mm, mod_ready, wv_turned, wv_t_ready = (sem(n) for n in ("silu_s", "mod_mm", "mod_ready", "wv_turned", "wv_t_ready"))
        u_mm, u_full_s, u_ready, rows_mm, rows_ready = (sem(n) for n in ("u_mm", "u_full_s", "u_ready", "rows_mm", "rows_ready"))
        qk_full_s, qk_w_ready, bias_mm, bias_ready, wide_ready = (
            sem(n) for n in ("qk_full_s", "qk_w_ready", "bias_mm", "bias_ready", "wide_ready"))
        w_turned, w1t_s, w2t_hi_s, ffn_w_ready, pick_ready, b1_mm = (
            sem(n) for n in ("w_turned", "w1t_s", "w2t_hi_s", "ffn_w_ready", "pick_ready", "b1_mm"))
        route_ones = sem("route_ones")
        stats, power_s, xn_ready = sem("stats"), sem("power_s"), sem("xn_ready")
        dve_step, pool_step = sem("dve_step"), sem("pool_step")
        xt_mm, h_hi_s, h_lo_s = sem("xt_mm"), sem("h_hi_s"), sem("h_lo_s")
        q_mm, k_mm, v_mm = sem("q_mm"), sem("k_mm"), sem("v_mm")
        q_hi_s, k_hi_s, v_hi_s = sem("q_hi_s"), sem("k_hi_s"), sem("v_hi_s")
        q_lo_s, k_lo_s, v_lo_s = sem("q_lo_s"), sem("k_lo_s"), sem("v_lo_s")
        xb_ready = sem("xb_ready")
        scored, nmax_ready, exp_done = sem("scored"), sem("nmax_ready"), sem("exp_done")
        turned, pt_hi_s = sem("turned"), sem("pt_hi_s")
        pt_lo_dve, pt_lo_pool, pv_done = sem("pt_lo_dve"), sem("pt_lo_pool"), sem("pv_done")
        rden_ready, ctx_out, ctx_turned, x1_ready = sem("rden_ready"), sem("ctx_out"), sem("ctx_turned"), sem("x1_ready")
        logits_mm, nmask_ready, nmask_turned, route_ready = (
            sem(n) for n in ("logits_mm", "nmask_ready", "nmask_turned", "route_ready"))
        hid_mm, hid_hi_s, hid_lo_s, y_mm, y_out, y_turned, res_ready = (
            sem(n) for n in ("hid_mm", "hid_hi_s", "hid_lo_s", "y_mm", "y_out", "y_turned", "res_ready"))

        x_tiles = x_in.rearrange("b (g i p) d -> g p (b i) d", p=P, i=GT)
        out_tiles = out.rearrange("b (g i p) d -> g p (b i) d", p=P, i=GT)
        col = lambda v: v.rearrange("(p o) -> p o", o=1)

        def grp(a, g):
            return a[:, g * GW:(g + 1) * GW]

        def tile(a, n):
            return a[:, n * P:(n + 1) * P]

        block = ctx.enter_context(nc.Block())

        @block.sync
        def _(sp):
            sp.dma_start(x[:, 0:GT, :], x_tiles[0]).then_inc(x_in_s[0], 16)
            sp.dma_start(wq[:], wq_in).then_inc(wqk_in_s, 16)
            sp.dma_start(wk[:], wk_in).then_inc(wqk_in_s, 16)
            for g in range(1, NG):
                sp.dma_start(x[:, g * GT:(g + 1) * GT, :], x_tiles[g]).then_inc(x_in_s[g], 16)
            sp.dma_start(w1, w1_in.rearrange("(m p) d -> p m d", p=P)).then_inc(ffn_in_s, 16)
            sp.dma_start(w2, w2_in).then_inc(ffn_in_s, 16)
            sp.dma_start(wr[:], wr_in).then_inc(ffn_in_s, 16)
            br_row = br_in.rearrange("(o n) -> o n", o=1)
            for i in range(GT):
                sp.dma_start(br[:, i, :], br_row.broadcast_to([P, NBLK])).then_inc(ffn_in_s, 16)
            sp.dma_start(b1[:], b1_in.rearrange("(o n) -> o n", o=1).broadcast_to([P, HID])).then_inc(b1_in_s, 16)
            for g in range(NG):
                sp.wait_ge(res_ready, g + 1)
                sp.dma_start(out_tiles[g], res[:, g % 2, :].rearrange("p (i d) -> p i d", i=GT)).then_inc(stored[g], 16)
            for g in range(NG):
                sp.wait_ge(stored[g], 16)

        @block.gpsimd
        def _(pool):
            steps = [0]

            def step(ins):
                steps[0] += 1
                ins.then_inc(pool_step, 1)
                pool.wait_ge(pool_step, steps[0])

            def power(n):
                k, s = n // NG, slice(n % NG * GT, n % NG * GT + GT)
                pool.wait_ge(stats, n + 1)
                pool.tensor_tensor(rstd[:, k, s], rstd[:, k, s], pow_half[:], ALU.pow).then_inc(power_s, 1)

            def low(lo, full, hi, done):
                pool.tensor_tensor(lo[:], full[:], hi[:].bitcast(F32), ALU.subtract).then_inc(done, 1)

            step(pool.memset(pow_half[:], -0.5))
            power(0)
            step(pool.memset(ident[:], 0.0))
            step(pool.affine_select(out=ident[:], in_=ident[:], compare_op=ALU.not_equal, fill=1.0, base=0,
                                    pattern=[[-1, P]], channel_multiplier=1))
            pool.tensor_copy(ident_b[:], ident[:]).then_inc(consts_made, 1)
            step(pool.memset(causal[:], 0.0))
            pool.affine_select(out=causal[:], in_=causal[:], compare_op=ALU.is_ge, fill=FAR, base=0,
                               pattern=[[-1, P]], channel_multiplier=1).then_inc(consts_made, 1)
            power(1)
            pool.wait_ge(qk_full_s, 1)
            low(wq_lo, wq_full, wq_hi, qk_w_ready)
            pool.wait_ge(qk_full_s, 2)
            low(wk_lo, wk_full, wk_hi, qk_w_ready)
            pool.wait_ge(u_full_s, 1)
            low(u_lo, u_full, u_hi, u_ready)
            power(2)
            step(pool.memset(pick[:], 1.0))
            step(pool.affine_select(out=pick[:], in_=pick[:], compare_op=ALU.is_ge, fill=0.0, base=0,
                                    pattern=[[1, HID]], channel_multiplier=-BLK))
            step(pool.affine_select(out=pick[:], in_=pick[:], compare_op=ALU.is_ge, fill=0.0, base=BLK - 1,
                                    pattern=[[-1, HID]], channel_multiplier=BLK))
            power(3)
            pool.memset(keys[:], 1.0)
            pool.memset(route[:], 1.0).then_inc(route_ones, 1)
            pool.wait_ge(rows_ready, 1)
            for g in range(NG):
                s = slice(g * GT, (g + 1) * GT)
                pool.wait_ge(xn_ready, g + 1)
                pool.tensor_tensor(x[:, s, :], x[:, s, :],
                                   gbo_row[:].rearrange("p (o d) -> p o d", o=1).broadcast_to([P, GT, D]),
                                   ALU.add).then_inc(xb_ready, 1)
            pool.wait_ge(xb_ready, NG)
            pool.wait_ge(b1_full_s, 1)
            for k, r in enumerate((32, 64, 96)):
                a = slice(r, r + 1)
                if k:
                    step(pool.tensor_copy(b1_part[:], b1[:]))
                    step(pool.tensor_tensor(b1[:], b1[:], b1_part[:], ALU.subtract))
                pool.tensor_copy(pick[a, :], b1[a, :]).then_inc(pick_ready, 1)
                pool.wait_ge(pick_ready, k + 1)

            def key_low(t):
                s, w = t % RING, pt_cols[t]
                pool.wait_ge(pt_hi_s, t + 1)
                if t >= RING:
                    pool.wait_ge(pv_done, t - RING + 1)
                pool.tensor_tensor(pt_lo[:, s, w:], pt_full[:, splits_before(t, True) % 2, w:],
                                   pt_hi[:, s, w:].bitcast(F32), ALU.subtract).then_inc(pt_lo_pool, 1)

            run(GPSIMD_PLAN, {"p": power, "t": key_low})

        @block.scalar
        def _(act):
            act.dma_start(cols[:, C:C + 1], c_in.rearrange("o p -> p o")).then_inc(c_in_s, 16)
            act.dma_start(wmod, wmod_in).then_inc(mod_in_s, 16)
            act.dma_start(wv[:], wv_in).then_inc(wvo_in_s, 16)
            act.dma_start(wo[:], wo_in).then_inc(wvo_in_s, 16)
            for n, v in ((BQ, bq_in), (BK, bk_in), (BV, bv_in), (BO, bo_in), (B2, b2_in)):
                act.dma_start(cols[:, n:n + 1], col(v)).then_inc(cols_in_s, 16)
            act.wait_ge(c_in_s, 16)
            nc.scalar.activation(silu[:, 0:1], cols[:, C:C + 1], ACT.Exp, scale=-1.0).then_inc(silu_s, 1)
            act.wait_ge(wv_turned, 1)
            nc.scalar.copy(wv_t[:], score_bank[1][:, 0:P]).then_inc(wv_t_ready, 1)

            def norm_high(n):
                act.wait_ge(xt_mm, n + 1)
                if n == NG:
                    act.wait_ge(v_mm, NG)
                nc.scalar.copy(grp(h_hi, n % NG), misc_bank[:]).then_inc(h_hi_s, 1)

            def q_high(g):
                act.wait_ge(q_mm, g + 1)
                if g == 0:
                    act.wait_ge(bias_ready, 1)
                nc.scalar.activation(grp(q_hi, g), turn_bank[0][:], ACT.Identity, bias=qk_bias[:, 0:1]).then_inc(q_hi_s, 1)

            def k_high(g):
                act.wait_ge(k_mm, g + 1)
                nc.scalar.activation(grp(k_hi, g), turn_bank[1][:], ACT.Identity, bias=qk_bias[:, 1:2]).then_inc(k_hi_s, 1)

            def v_high(g):
                act.wait_ge(v_mm, g + 1)
                nc.scalar.copy(grp(v_hi, g), ctx_bank[:]).then_inc(v_hi_s, 1)

            def exps(k):
                g, r, c = chunk_of[k]
                n, w = g * GT + r, chunk_width(g, r, c)
                if c == 0:
                    act.wait_ge(nmax_ready, n + 1)
                    if r == 0 and g == 1:
                        act.wait_ge(w_turned, 2)
                    if r == 0 and g >= 2:
                        act.wait_ge(turned, key_no(g - 1, 0))
                nc.scalar.activation(probs[g % 2][:, r, c * GW:c * GW + w],
                                     score_bank[k % 4][:, 0:w], ACT.Exp, bias=nmax[:, n:n + 1],
                                     accum_out=dpart[:, n, c:c + 1]).then_inc(exp_done, 1)

            def key_high(t):
                s, w = t % RING, pt_cols[t]
                act.wait_ge(turned, t + 1)
                if pool_splits(t):
                    n = splits_before(t, True)
                    if n >= 2:
                        act.wait_ge(pt_lo_pool, n - 1)
                    nc.scalar.copy(pt_full[:, n % 2, w:], turn_bank[t % 2][:, w:])
                if t >= RING:
                    act.wait_ge(pv_done, t - RING + 1)
                nc.scalar.copy(pt_hi[:, s, w:], turn_bank[t % 2][:, w:]).then_inc(pt_hi_s, 1)

            def ctx_copy(g):
                act.wait_ge(pv_done, key_no(g + 1, 0))
                if g >= 1:
                    act.wait_ge(ctx_turned, g)
                else:
                    act.wait_ge(gate_ready, 1)
                nc.scalar.activation(ctx_sb[:], ctx_bank[:], ACT.Identity, scale=gate[:, GA:GA + 1]).then_inc(ctx_out, 1)

            def route_copy(g):
                act.wait_ge(nmask_turned, g + 1)
                if g == 0:
                    act.wait_ge(route_ones, 1)
                nc.scalar.copy(route[0:NBLK, g * GW:(g + 1) * GW],
                               misc_bank[0:NBLK, 0:GW // 2].bitcast(BF16)).then_inc(route_ready, 1)

            def hidden(n):
                g, m = n // NH, n % NH
                act.wait_ge(hid_mm, g * NH + m + 1)
                if g >= 1:
                    act.wait_ge(y_mm, (g - 1) * NH + m + 1)
                nc.scalar.activation(hid_hi[:, m, :], score_bank[(CHUNKS + g * NH + m) % 4][:], ACT.Relu).then_inc(hid_hi_s, 1)

            def y_copy(g):
                act.wait_ge(y_mm, NH * (g + 1))
                if g >= 1:
                    act.wait_ge(y_turned, g)
                nc.scalar.activation(y_sb[:], turn_bank[g % 2][:], ACT.Identity, bias=gbb2[:],
                                     scale=gate[:, GB:GB + 1]).then_inc(y_out, 1)

            norm_high(0)
            for high in (q_high, k_high, v_high):
                high(0)
            norm_high(1)
            act.wait_ge(w_turned, 1)
            nc.scalar.copy(w1t_full[:], score_bank[0][:]).then_inc(w1t_s, 1)
            act.wait_ge(w_turned, 2)
            nc.scalar.copy(w2t_hi[:], score_bank[1][:]).then_inc(w2t_hi_s, 1)
            for high in (q_high, k_high, v_high):
                high(1)
            run(SCALAR_PLAN, {"n": norm_high, "q": q_high, "k": k_high, "v": v_high, "e": exps, "t": key_high,
                              "c": ctx_copy, "m": route_copy, "h": hidden, "y": y_copy})

        @block.vector
        def _(dve):
            steps = [0]

            def step(ins):
                steps[0] += 1
                ins.then_inc(dve_step, 1)
                dve.wait_ge(dve_step, steps[0])

            def norm_stats(n):
                k, g = n // NG, n % NG
                s = slice(g * GT, (g + 1) * GT)
                if k == 0:
                    dve.wait_ge(x_in_s[g], 16)
                else:
                    dve.wait_ge(x1_ready, g + 1)
                for i in range(GT):
                    last = nc.vector.bn_stats(st[:, k, g * GT + i, :], x[:, g * GT + i, :])
                step(last)
                for i in range(GT):
                    last = nc.vector.bn_aggr(mv[:, k, g * GT + i, :], st[:, k, g * GT + i, :])
                step(last)
                nc.vector.tensor_scalar(rstd[:, k, s], mv[:, k, s, 1], EPS, None, ALU.add).then_inc(stats, 1)

            def apply(n):
                k, g = n // NG, n % NG
                dve.wait_ge(power_s, n + 1)
                if n >= 2:
                    dve.wait_ge(xt_mm, n - 1)
                for i in range(GT):
                    t = g * GT + i
                    last = nc.vector.tensor_scalar(xn[:, n % 2, i, :], x[:, t, :], mv[:, k, t, 0:1],
                                                   rstd[:, k, t:t + 1], ALU.subtract, ALU.mult)
                last.then_inc(xn_ready, 1)

            def norm_low(n):
                dve.wait_ge(h_hi_s, n + 1)
                nc.vector.tensor_tensor(grp(h_lo, n % NG), misc_bank[:], grp(h_hi, n % NG).bitcast(F32),
                                        ALU.subtract).then_inc(h_lo_s, 1)

            def qk_low(g, n, hi_s, lo_s, hi, lo):
                dve.wait_ge(hi_s, g + 1)
                nc.vector.scalar_tensor_tensor(out=grp(lo, g), in0=turn_bank[n][:], scalar=qk_bias[:, n:n + 1],
                                               in1=grp(hi, g).bitcast(F32), op0=ALU.add,
                                               op1=ALU.subtract).then_inc(lo_s, 1)

            def low_q(g):
                qk_low(g, 0, q_hi_s, q_lo_s, q_hi, q_lo)

            def low_k(g):
                qk_low(g, 1, k_hi_s, k_lo_s, k_hi, k_lo)

            def low_v(g):
                dve.wait_ge(v_hi_s, g + 1)
                nc.vector.tensor_tensor(grp(v_lo, g), ctx_bank[:], grp(v_hi, g).bitcast(F32),
                                        ALU.subtract).then_inc(v_lo_s, 1)

            def row_max(k):
                g, r, c = chunk_of[k]
                n, w = g * GT + r, chunk_width(g, r, c)
                dve.wait_ge(scored, k + 1)
                if g == 0:
                    nc.vector.tensor_reduce(nmax[:, n:n + 1], score_bank[k % 4][:, 0:w], AX.X, ALU.max,
                                            negate=True).then_inc(nmax_ready, 1)
                    return
                last = nc.vector.tensor_reduce(cmax[:, n, c:c + 1], score_bank[k % 4][:, 0:w], AX.X, ALU.max)
                if c == g:
                    step(last)
                    nc.vector.tensor_reduce(nmax[:, n:n + 1], cmax[:, n, 0:g + 1], AX.X, ALU.max,
                                            negate=True).then_inc(nmax_ready, 1)

            def key_low(t):
                s, w = t % RING, pt_cols[t]
                dve.wait_ge(pt_hi_s, t + 1)
                if t >= RING:
                    dve.wait_ge(pv_done, t - RING + 1)
                nc.vector.tensor_tensor(pt_lo[:, s, w:], turn_bank[t % 2][:, w:], pt_hi[:, s, w:].bitcast(F32),
                                        ALU.subtract).then_inc(pt_lo_dve, 1)

            def row_sums(g):
                s = slice(g * GT, (g + 1) * GT)
                dve.wait_ge(exp_done, chunk_no(g + 1, 0, 0))
                step(nc.vector.tensor_reduce(den[:, s], dpart[:, s, 0:g + 1], AX.X, ALU.add))
                step(nc.vector.reciprocal(rden[:, s], den[:, s]))

            def attention_out(g):
                row_sums(g)
                dve.wait_ge(ctx_turned, g + 1)
                dve.wait_ge(xb_ready, g + 1)
                for i in range(GT):
                    t = g * GT + i
                    last = nc.vector.scalar_tensor_tensor(out=x[:, t, :], in0=tile(misc_bank, i),
                                                          scalar=rden[:, t:t + 1], in1=x[:, t, :],
                                                          op0=ALU.mult, op1=ALU.add)
                last.then_inc(x1_ready, 1)
                norm_stats(NG + g)

            def choose(g):
                dve.wait_ge(logits_mm, g + 1)
                if g == 0:
                    dve.wait_ge(route_ones, 1)
                step(nc.vector.tensor_tensor(logit[:], misc_bank[:, 0:GT * NBLK].rearrange("p (i e) -> p i e", i=GT),
                                             br[:], ALU.add))
                step(nc.vector.tensor_reduce(lmax[:], logit[:], AX.X, ALU.max))
                step(nc.vector.tensor_tensor(ldiff[:], logit[:],
                                             lmax[:].rearrange("p (i o) -> p i o", o=1).broadcast_to([P, GT, NBLK]),
                                             ALU.subtract))
                step(nc.vector.tensor_scalar(keys[:, :, 0:NBLK], ldiff[:], UNDER, None, ALU.max))
                for i in range(GT):
                    last = nc.vector.max(top8[:, i, :], keys[:, i, :])
                step(last)
                for i in range(GT):
                    last = nc.vector.match_replace(marked[:, i, :], top8[:, i, :], keys[:, i, :], 1.0)
                step(last)
                if g >= 1:
                    dve.wait_ge(nmask_turned, g)
                nc.vector.tensor_scalar(nmask[:], marked[:, :, 0:NBLK], 0.0, FAR, ALU.is_le, ALU.mult).then_inc(nmask_ready, 1)

            def hidden(n):
                g, m = n // NH, n % NH
                dve.wait_ge(hid_hi_s, n + 1)
                if g >= 1:
                    dve.wait_ge(y_mm, (g - 1) * NH + m + 1)
                nc.vector.scalar_tensor_tensor(out=hid_lo[:, m, :], in0=score_bank[(CHUNKS + n) % 4][:], scalar=0.0,
                                               in1=hid_hi[:, m, :].bitcast(F32), op0=ALU.max,
                                               op1=ALU.subtract).then_inc(hid_lo_s, 1)

            def finish(g):
                dve.wait_ge(y_turned, g + 1)
                if g >= 2:
                    dve.wait_ge(stored[g - 2], 16)
                nc.vector.tensor_tensor(res[:, g % 2, :], ctx_bank[:],
                                        x[:, g * GT:(g + 1) * GT, :].rearrange("p i d -> p (i d)"),
                                        ALU.add).then_inc(res_ready, 1)

            norm_stats(0)
            dve.wait_ge(silu_s, 1)
            step(nc.vector.tensor_scalar(silu[:, 1:2], silu[:, 0:1], 1.0, None, ALU.add))
            step(nc.vector.reciprocal(silu[:, 2:3], silu[:, 1:2]))
            nc.vector.tensor_tensor(silu[:, 3:4], silu[:, 2:3], cols[:, C:C + 1], ALU.mult).then_inc(silu_s, 1)
            apply(0)
            norm_stats(1)
            dve.wait_ge(mod_mm, 1)
            nc.vector.tensor_copy(mod[:], score_bank[0][:, 0:6]).then_inc(mod_ready, 1)
            dve.wait_ge(mod_ready, 1)
            nc.vector.tensor_scalar(gate[:, CA:CA + 1], mod[:, CA:CA + 1], 1.0, None, ALU.add)
            step(nc.vector.tensor_scalar(gate[:, CB:CB + 1], mod[:, CB:CB + 1], 1.0, None, ALU.add))
            dve.wait_ge(wqk_in_s, 32)
            for w, full, hi, scale in ((wq, wq_full, wq_hi, QSCALE), (wk, wk_full, wk_hi, 1.0)):
                nc.vector.tensor_scalar(full[:], w[:], gate[:, CA:CA + 1], scale, ALU.mult, ALU.mult)
                nc.vector.tensor_scalar(hi[:], w[:], gate[:, CA:CA + 1], scale, ALU.mult, ALU.mult).then_inc(qk_full_s, 1)
            norm_low(0)
            dve.wait_ge(bias_mm, 1)
            dve.wait_ge(cols_in_s, 80)
            nc.vector.tensor_scalar(qk_bias[:, 0:1], score_bank[3][:, 0:1], cols[:, BQ:BQ + 1], QSCALE, ALU.add, ALU.mult)
            nc.vector.tensor_scalar(v_bias[:, 0:1], score_bank[3][:, 2:3], cols[:, BV:BV + 1], None, ALU.add)
            nc.vector.tensor_scalar(qk_bias[:, 1:2], score_bank[3][:, 1:2], cols[:, BK:BK + 1], None, ALU.add).then_inc(bias_ready, 1)
            dve.wait_ge(u_mm, 1)
            nc.vector.tensor_scalar(u_full[:], score_bank[2][:, 0:P], gate[:, CA:CA + 1], None, ALU.mult)
            nc.vector.tensor_scalar(u_hi[:], score_bank[2][:, 0:P], gate[:, CA:CA + 1], None, ALU.mult).then_inc(u_full_s, 1)
            apply(1)
            for s, sign in ((GA, SA), (GB, SB_)):
                step(nc.vector.tensor_scalar(gate[:, sign:sign + 1], mod[:, s:s + 1], 0.0, 2.0, ALU.is_ge, ALU.mult))
                step(nc.vector.tensor_scalar(gate[:, sign:sign + 1], gate[:, sign:sign + 1], -1.0, None, ALU.add))
                step(nc.vector.tensor_scalar(gate[:, s:s + 1], mod[:, s:s + 1], gate[:, sign:sign + 1], 0.25,
                                             ALU.mult, ALU.max))
                step(nc.vector.tensor_scalar(gate[:, s:s + 1], gate[:, s:s + 1], gate[:, sign:sign + 1], None, ALU.mult))
            nc.vector.tensor_scalar(gbb2[:], gate[:, GB:GB + 1], cols[:, B2:B2 + 1], None, ALU.mult).then_inc(gate_ready, 1)
            for low in (low_q, low_k, low_v):
                low(0)
            norm_stats(2)
            norm_low(1)
            dve.wait_ge(bias_mm, 2)
            step(nc.vector.tensor_scalar(v_bias[:, 1:2], score_bank[3][:, 4:5], cols[:, BO:BO + 1], gate[:, GA:GA + 1],
                                         ALU.add, ALU.mult))
            dve.wait_ge(consts_made, 1)
            nc.vector.tensor_scalar(gbo_wide[:], ident[:], 0.0, v_bias[:, 1:2], ALU.mult, ALU.add)
            nc.vector.tensor_scalar(shift_wide[:], ident[:], 0.0, mod[:, SB_:SB_ + 1], ALU.mult, ALU.add).then_inc(wide_ready, 1)
            dve.wait_ge(w1t_s, 1)
            nc.vector.tensor_scalar(w1t_hi[:], w1t_full[:], gate[:, CB:CB + 1], None, ALU.mult).then_inc(w1t_s, 1)
            dve.wait_ge(w1t_s, 2)
            nc.vector.scalar_tensor_tensor(out=w1t_lo[:], in0=w1t_full[:], scalar=gate[:, CB:CB + 1],
                                           in1=w1t_hi[:].bitcast(F32), op0=ALU.mult, op1=ALU.subtract)
            dve.wait_ge(w2t_hi_s, 1)
            nc.vector.tensor_tensor(w2t_lo[:], score_bank[1][:], w2t_hi[:].bitcast(F32), ALU.subtract)
            nc.vector.tensor_scalar(wr_full[:], wr[:], gate[:, CB:CB + 1], None, ALU.mult)
            step(nc.vector.tensor_scalar(wr_hi[:], wr[:], gate[:, CB:CB + 1], None, ALU.mult))
            nc.vector.tensor_tensor(wr_lo[:], wr_full[:], wr_hi[:].bitcast(F32), ALU.subtract).then_inc(ffn_w_ready, 1)
            apply(2)
            dve.wait_ge(rows_mm, 1)
            nc.vector.tensor_copy(gbo_row[:], score_bank[2][:, P:2 * P]).then_inc(rows_ready, 1)
            nc.vector.tensor_tensor(br[:], br[:], score_bank[2][:, 2 * P:2 * P + NBLK].rearrange("p (o e) -> p o e", o=1)
                                    .broadcast_to([P, GT, NBLK]), ALU.add).then_inc(rows_ready, 1)
            for low in (low_q, low_k, low_v):
                low(1)
            dve.wait_ge(b1_mm, 1)
            dve.wait_ge(b1_in_s, 16)
            nc.vector.tensor_tensor(b1[:], b1[:], score_bank[3][:], ALU.add).then_inc(b1_full_s, 1)
            norm_stats(3)
            run(VECTOR_PLAN, {"a": apply, "n": norm_low, "q": low_q, "k": low_k, "v": low_v, "s": row_max,
                              "t": key_low, "x": attention_out, "m": choose, "h": hidden, "f": finish})

        @block.tensor
        def _(pe):
            mm = nc.tensor.matmul

            def three(dst, w_hi, w_lo, m_hi, m_lo, hi_wait=None, lo_wait=None, start=True, stop=True):
                if hi_wait:
                    pe.wait_ge(*hi_wait)
                mm(dst, w_hi, m_hi, start=start, stop=False)
                mm(dst, w_lo, m_hi, start=False, stop=False)
                if lo_wait:
                    pe.wait_ge(*lo_wait)
                return mm(dst, w_hi, m_lo, start=False, stop=stop)

            def turn_norm(n):
                pe.wait_ge(xn_ready, n + 1)
                if 1 <= n < NG:
                    pe.wait_ge(h_lo_s, n)
                elif n >= NG:
                    pe.wait_ge(x1_ready, n - NG + 1)
                for i in range(GT):
                    last = nc.tensor.transpose(tile(misc_bank, i), xn[:, n % 2, i, :], ident[:])
                last.then_inc(xt_mm, 1)

            def project_q(g):
                pe.wait_ge(qk_w_ready, 1)
                if g >= 1:
                    pe.wait_ge(q_lo_s, g)
                three(turn_bank[0][:], wq_hi[:], wq_lo[:], grp(h_hi, g), grp(h_lo, g),
                      (h_hi_s, g + 1), (h_lo_s, g + 1)).then_inc(q_mm, 1)

            def project_k(g):
                pe.wait_ge(qk_w_ready, 2)
                if g >= 1:
                    pe.wait_ge(k_lo_s, g)
                three(turn_bank[1][:], wk_hi[:], wk_lo[:], grp(h_hi, g), grp(h_lo, g),
                      (h_hi_s, g + 1), (h_lo_s, g + 1)).then_inc(k_mm, 1)

            def project_v(g):
                pe.wait_ge(u_ready, 1)
                pe.wait_ge(h_lo_s, g + 1)
                if g >= 1:
                    pe.wait_ge(v_lo_s, g)
                for n in range(g * GT, (g + 1) * GT):
                    last = three(tile(ctx_bank, n % GT), tile(h_hi, n), tile(h_lo, n), u_hi[:], u_lo[:])
                last.then_inc(v_mm, 1)

            def score(k):
                g, r, c = chunk_of[k]
                w, t = chunk_width(g, r, c), g * GT + r
                if k >= 4:
                    pe.wait_ge(exp_done, k - 3)
                if c == 0 and r == 0:
                    pe.wait_ge(q_lo_s, g + 1)
                    pe.wait_ge(k_lo_s, g + 1)
                last = three(score_bank[k % 4][:, 0:w], tile(q_hi, t), tile(q_lo, t), k_hi[:, c * GW:c * GW + w],
                             k_lo[:, c * GW:c * GW + w], stop=(c < g))
                if c == g:
                    last = mm(score_bank[k % 4][:, w - P:w], ident_b[:], causal[:], start=False, stop=True)
                last.then_inc(scored, 1)

            def turn_keys(t):
                g, j = key_of[t]
                pe.wait_ge(exp_done, chunk_no(g, GT - 1, j // GT) + 1)
                if t < 2:
                    pe.wait_ge((q_lo_s, k_lo_s)[t], NG)
                elif pool_splits(t - 2):
                    pe.wait_ge(pt_hi_s, t - 1)
                else:
                    pe.wait_ge(pt_lo_dve, splits_before(t - 2, False) + 1)
                for r in range(key_from(g, j), GT):
                    last = nc.tensor.transpose(turn_bank[t % 2][:, r * P:(r + 1) * P],
                                               probs[g % 2][:, r, j * P:(j + 1) * P], ident[:])
                last.then_inc(turned, 1)

            def weigh(t):
                g, j = key_of[t]
                last_j = GT * (g + 1) - 1
                s, w = t % RING, pt_cols[t]
                by_pool = pool_splits(t)
                if j == 0:
                    if g == 0:
                        pe.wait_ge(v_lo_s, NG)
                    else:
                        pe.wait_ge(ctx_out, g)
                three(ctx_bank[:, w:], tile(v_hi, j), tile(v_lo, j), pt_hi[:, s, w:], pt_lo[:, s, w:],
                      (pt_hi_s, t + 1), (pt_lo_pool if by_pool else pt_lo_dve, splits_before(t, by_pool) + 1),
                      start=(j == 0), stop=(j == last_j)).then_inc(pv_done, 1)

            def turn_context(g):
                pe.wait_ge(ctx_out, g + 1)
                if g == 0:
                    pe.wait_ge(h_lo_s, NG)
                else:
                    pe.wait_ge(route_ready, g)
                for i in range(GT):
                    last = nc.tensor.transpose(tile(misc_bank, i), tile(ctx_sb, i), ident[:])
                last.then_inc(ctx_turned, 1)

            def router(g):
                pe.wait_ge(h_lo_s, NG + g + 1)
                if g == 0:
                    pe.wait_ge(ffn_w_ready, 1)
                for i in range(GT):
                    last = three(misc_bank[:, i * NBLK:(i + 1) * NBLK], tile(h_hi, g * GT + i), tile(h_lo, g * GT + i),
                                 wr_hi[:], wr_lo[:])
                last.then_inc(logits_mm, 1)

            def turn_mask(g):
                pe.wait_ge(nmask_ready, g + 1)
                for i in range(GT):
                    last = nc.tensor.transpose(misc_bank[0:NBLK, i * P // 2:(i + 1) * P // 2].bitcast(BF16),
                                               nmask[:, i, :], ident_b[:])
                last.then_inc(nmask_turned, 1)

            def hidden(n):
                g, m = n // NH, n % NH
                if n < 4:
                    pe.wait_ge(exp_done, CHUNKS - 3 + n)
                else:
                    pe.wait_ge(hid_lo_s, n - 3)
                if n == 0:
                    pe.wait_ge(pick_ready, 3)
                if m == 0:
                    pe.wait_ge(route_ready, g + 1)
                    pe.wait_ge(h_lo_s, NG + g + 1)
                dst = score_bank[(CHUNKS + n) % 4][:]
                three(dst, tile(w1t_hi, m), tile(w1t_lo, m), grp(h_hi, g), grp(h_lo, g), stop=False)
                mm(dst, tile(pick, m), grp(route, g), start=False, stop=True).then_inc(hid_mm, 1)

            def down(n):
                g, m = n // NH, n % NH
                if m == 0:
                    if g < 2:
                        pe.wait_ge(pt_lo_dve, splits_before(len(pt_cols), False))
                        pe.wait_ge(pt_hi_s, len(pt_cols))
                    else:
                        pe.wait_ge(y_out, g - 1)
                three(turn_bank[g % 2][:], tile(w2t_hi, m), tile(w2t_lo, m), hid_hi[:, m, :], hid_lo[:, m, :],
                      (hid_hi_s, n + 1), (hid_lo_s, n + 1), start=(m == 0), stop=(m == NH - 1)).then_inc(y_mm, 1)

            def turn_y(g):
                pe.wait_ge(y_out, g + 1)
                if g == 0:
                    pe.wait_ge(ctx_out, NG)
                else:
                    pe.wait_ge(res_ready, g)
                for i in range(GT):
                    last = nc.tensor.transpose(tile(ctx_bank, i), tile(y_sb, i), ident[:])
                last.then_inc(y_turned, 1)

            pe.wait_ge(consts_made, 1)
            pe.wait_ge(wvo_in_s, 32)
            nc.tensor.transpose(score_bank[1][:, 0:P], wv[:], ident[:]).then_inc(wv_turned, 1)
            pe.wait_ge(silu_s, 2)
            pe.wait_ge(mod_in_s, 16)
            for n in range(6):
                last = mm(score_bank[0][:, n:n + 1], tile(wmod, n), silu[:, 3:4], start=True, stop=True)
            last.then_inc(mod_mm, 1)
            turn_norm(0)
            pe.wait_ge(wv_t_ready, 1)
            mm(score_bank[2][:, 0:P], wv_t[:], wo[:], start=True, stop=True).then_inc(u_mm, 1)
            pe.wait_ge(mod_ready, 1)
            pe.wait_ge(wqk_in_s, 32)
            for n, w in enumerate((wq, wk, wv)):
                last = mm(score_bank[3][:, n:n + 1], w[:], mod[:, SA:SA + 1], start=True, stop=True)
            last.then_inc(bias_mm, 1)
            for project in (project_q, project_k, project_v):
                project(0)
            turn_norm(1)
            pe.wait_ge(bias_ready, 1)
            mm(score_bank[3][:, 4:5], wo[:], v_bias[:, 0:1], start=True, stop=True).then_inc(bias_mm, 1)
            pe.wait_ge(ffn_in_s, 16 * (3 + GT))
            for m in range(NH):
                last = nc.tensor.transpose(tile(score_bank[0], m), w1[:, m, :], ident[:])
            last.then_inc(w_turned, 1)
            for m in range(NH):
                last = nc.tensor.transpose(tile(score_bank[1], m), tile(w2, m), ident[:])
            last.then_inc(w_turned, 1)
            for project in (project_q, project_k, project_v):
                project(1)
            pe.wait_ge(wide_ready, 1)
            pe.wait_ge(u_full_s, 1)
            mm(score_bank[2][:, P:2 * P], gbo_wide[:], ident[:], start=True, stop=True)
            mm(score_bank[2][:, 2 * P:2 * P + NBLK], shift_wide[:], wr[:], start=True, stop=True).then_inc(rows_mm, 1)
            pe.wait_ge(w1t_s, 1)
            mm(score_bank[3][:], shift_wide[:], w1t_full[:], start=True, stop=True).then_inc(b1_mm, 1)
            turn_norm(2)
            pe.wait_ge(ffn_w_ready, 1)
            pe.wait_ge(rows_ready, 2)
            pe.wait_ge(b1_full_s, 1)
            pe.wait_ge(consts_made, 2)
            run(TENSOR_PLAN, {"n": turn_norm, "q": project_q, "k": project_k, "v": project_v, "s": score,
                              "t": turn_keys, "w": weigh, "c": turn_context, "r": router, "m": turn_mask,
                              "h": hidden, "d": down, "y": turn_y})


_INS = ['L0_attn_y_all', 'L0_attn_Wq', 'L0_attn_bq', 'L0_attn_Wk', 'L0_attn_bk', 'L0_attn_Wv', 'L0_attn_bv',
        'L0_attn_Wo', 'L0_attn_bo', 'L0_ffn_w_router', 'L0_ffn_b_router', 'L0_ffn_w1', 'L0_ffn_b1', 'L0_ffn_w2',
        'L0_ffn_b2', 'L0_c', 'L0_wmod']
_OUTS = [((1, 2048, 128), 'float32')]


def kernel(**inputs):
    import numpy as _np
    import concourse.bacc as _bacc
    from concourse import mybir as _mybir
    from concourse.bass_utils import run_bass_kernel_spmd as _run

    nc = _bacc.Bacc("TRN2", target_bir_lowering=False, num_devices=1)
    arrays, args = {}, []
    for name in _INS:
        a = _np.ascontiguousarray(inputs[name])
        arrays[f"in_{name}_dram"] = a
        args.append(nc.dram_tensor(f"in_{name}_dram", a.shape, _mybir.dt.from_np(a.dtype), kind="ExternalInput").ap())
    for i, (shape, dtype) in enumerate(_OUTS):
        dt = _mybir.dt.from_np(_np.dtype(dtype))
        args.append(nc.dram_tensor(f"out_{i}_dram", shape, dt, kind="ExternalOutput").ap())
    adaln_attention_sparse_ffn(nc, *args)
    r = _run(nc, [arrays], core_ids=[0])
    got = tuple(r.results[0][f"out_{i}_dram"] for i in range(len(_OUTS)))
    return got[0]
```

```python
from contextlib import ExitStack

import concourse.bass as bass
from concourse import mybir

ALU = mybir.AluOpType
ACT = mybir.ActivationFunctionType
AX = mybir.AxisListType
F32 = mybir.dt.float32
F32R = mybir.dt.float32r
BF16 = mybir.dt.bfloat16


P = 128
GT = 4
GW = GT * P
EPS = 1e-5
FAR = -1e30
WAKE = 10
LATE = 6
RING = 6
SCALAR_NORMS = (1,)
VECTOR_NORMS = (0, 1, 2)
UNDER = -87.33

TENSOR_PLAN = """
i0 i1 i2 z1 z0 z2 n0 z3 i3 i4 i5 i6 i7 i8 i9 i10 i11 q0 n1 k0 v0 n2 q1 s0 s1 s2 s3 z5 k1 v1 z6 s4 s5 s6 q2 k2
z7 s7 v2 s8 t0 s9 t1 s10 s11 z8 t2 n3 t3 s12 s13 w0 w1 s14 t4 t5 s15 w2 w3 s16 t6 s17 c0 s18 v3 t7 s19 s20 s21
q3 k3 w4 w5 s22 s23 t8 n4 w6 w7 s24 w8 s25 s26 t9 s27 t10 r0 t11 t12 w9 s28 w10 s29 m0 t13 s30 w11 s31 t14 t15
w12 c1 w13 t16 w14 t17 s32 s33 s34 s35 t18 t19 n5 w15 w16 t20 t21 w17 w18 s36 s37 w19 s38 s39 t22 t23 r1 w20
w21 t24 t25 w22 w23 h0 m1 t26 t27 w24 h1 w25 t28 t29 c2 w26 w27 t30 t31 w28 w29 h2 t32 t33 w30 n6 w31 t34 t35
w32 w33 h3 t36 t37 r2 w34 h4 t38 t39 w35 w36 w37 m2 w38 w39 d0 d1 c3 d2 d3 d4 h5 h6 h7 d5 y0 n7 h8 d6 h9 h10
r3 d7 h11 d8 d9 d10 m3 y1 d11 h12 h13 y2 h14 h15 d12 d13 d14 d15 y3
"""
SCALAR_PLAN = """
z0 z4 z5 z1 n0 a1 z6 q0 n1 k0 v0 n2 q1 e0 k1 e1 e2 z2 v1 e3 q2 e4 z3 e5 k2 v2 e6 e7 t0 t1 e8 e9 t2 n3 e10 t3
e11 t4 e12 e13 c0 e14 t5 t6 e15 e16 e17 t7 v3 q3 e18 e19 e20 k3 t8 n4 e21 e22 e23 t9 t10 e24 e25 e26 e27 t11
t12 m0 t13 c1 t14 t15 e28 e29 e30 e31 t16 t17 t18 t19 n5 e32 e33 e34 e35 t20 t21 t22 t23 e36 e37 e38 t24 t25
c2 e39 t26 m1 t27 h0 t28 t29 h1 t30 t31 h2 t32 t33 n6 t34 t35 h3 t36 t37 t38 t39 m2 c3 h4 y0 h5 h6 h7 n7 h8 h9
h10 y1 h11 m3 y2 h12 h13 h14 h15 y3
"""
VECTOR_PLAN = """
g0 z0 a0 g1 z1 g2 z5 z12 n0 g3 a2 q0 n1 k0 z4 s0 q1 s1 z7 s2 k1 s3 n2 s4 z8 s5 a3 s6 q2 s7 k2 s8 z9 s9 t0 z10
s10 s11 t2 s12 s13 s14 t4 s15 s16 s17 x0 t6 s18 s19 s20 s21 q3 a4 s22 k3 s23 t8 s24 s25 s26 s27 t10 m0 s28 s29
t12 s30 s31 t14 x1 s32 t16 a5 s33 t18 s34 s35 s36 s37 t20 s38 s39 t22 m1 t24 t26 h0 t28 x2 t30 h1 a6 t32 h2
t34 h3 t36 m2 t38 h4 x3 h5 a7 h6 f0 h7 h8 h9 h10 m3 h11 f1 h12 f2 h13 h14 h15 f3
"""
GPSIMD_PLAN = """
z0 z1 p0 z2 z3 p1 p2 z4 z5 p3 z6 v0 z11 v1 z12 v2 t1 z7 n3 t3 z8 z9 z10 t5 z13 p4 t7 v3 n4 t9 t11 t13 t15 p5
t17 t19 n5 t21 t23 t25 t27 t29 p6 t31 t33 n6 t35 t37 t39 p7 n7
"""


def adaln_attention_sparse_ffn(nc, x_in, wq_in, bq_in, wk_in, bk_in, wv_in, bv_in, wo_in, bo_in,
                               wr_in, br_in, w1_in, b1_in, w2_in, b2_in, c_in, wmod_in, out):
    _, T, D = x_in.shape
    HID = w1_in.shape[0]
    NBLK = wr_in.shape[1]
    TOPK = NBLK // 4
    BLK = HID // NBLK
    NT = T // P
    NG = T // GW
    NH = HID // P
    PADS = 8 - TOPK
    KEYS = NBLK + PADS
    QSCALE = float(D) ** -0.5
    assert D == P and wq_in.shape[1] == P and HID == GW and NG == 4

    def chunk_no(g, r, c):
        return sum(GT * (k + 1) for k in range(g)) + r * (g + 1) + c

    def chunk_width(g, r, c):
        return GW if c < g else P * (r + 1)

    def key_no(g, j):
        return sum(GT * (k + 1) for k in range(g)) + j

    def key_from(g, j):
        return max(0, j - GT * g)

    CHUNKS = chunk_no(NG, 0, 0)
    chunk_of = [(g, r, c) for g in range(NG) for r in range(GT) for c in range(g + 1)]
    key_of = [(g, j) for g in range(NG) for j in range(GT * (g + 1))]
    pt_cols = [P * key_from(g, j) for g in range(NG) for j in range(GT * (g + 1))]

    def pool_splits(t):
        return t % 2 == 1

    def pool_lowers(n):
        return n not in VECTOR_NORMS

    def result_parts(g):
        return (slice(0, GW),) if g < NG - 1 else (slice(0, GW // 2), slice(GW // 2, GW))

    def scalar_applies(n):
        return n in SCALAR_NORMS

    def splits_before(t, by_pool):
        return sum(pool_splits(k) == by_pool for k in range(t))

    def run(plan, steps):
        for word in plan.split():
            steps[word[0]](int(word[1:]))

    with ExitStack() as ctx:
        def sb(name, shape, dt=F32):
            return ctx.enter_context(nc.sbuf_tensor(name, shape, dt))

        def sem(name):
            return ctx.enter_context(nc.semaphore(name))

        bank = [ctx.enter_context(nc.psum_tensor(f"bank{i}", [P, GW], F32)) for i in range(8)]
        score_bank = bank[0:4]
        turn_bank = bank[4:6]
        ctx_bank, misc_bank = bank[6], bank[7]
        result_bank = ctx_bank, misc_bank

        x = sb("x", [P, NT, D])
        xn = sb("xn", [P, 2, GT, D])
        h_hi = sb("h_hi", [P, T], F32R)
        h_lo = sb("h_lo", [P, T], F32R)
        h_full = sb("h_full", [P, 2, GW])
        q_hi = sb("q_hi", [P, T], F32R)
        q_lo = sb("q_lo", [P, T], F32R)
        k_hi = sb("k_hi", [P, T], F32R)
        k_lo = sb("k_lo", [P, T], F32R)
        v_hi = sb("v_hi", [P, T], F32R)
        v_lo = sb("v_lo", [P, T], F32R)
        probs = [sb("probs0", [P, GT, 3 * GW]), sb("probs1", [P, GT, 4 * GW])]
        pt_full = sb("pt_full", [P, 2, GW])
        v_full = sb("v_full", [P, GW])
        pt_hi = sb("pt_hi", [P, RING, GW], F32R)
        pt_lo = sb("pt_lo", [P, RING, GW], F32R)
        ctx_sb = sb("ctx_sb", [P, GW])
        hid_hi = q_hi[:].rearrange("p (m t) -> p m t", m=NH)
        hid_lo = q_lo[:].rearrange("p (m t) -> p m t", m=NH)
        y_sb = sb("y_sb", [P, GW])
        res = sb("res", [P, 2, GW])
        wq, wk, wv, wo = (sb(n, [P, P]) for n in ("wq", "wk", "wv", "wo"))
        wq_full = sb("wq_full", [P, P])
        wq_hi, wk_hi, u_hi = (sb(n, [P, P], F32R) for n in ("wq_hi", "wk_hi", "u_hi"))
        wq_lo, wk_lo, u_lo = (sb(n, [P, P], F32R) for n in ("wq_lo", "wk_lo", "u_lo"))
        wv_t = sb("wv_t", [P, P])
        u_full = sb("u_full", [P, P])
        gbo_wide = sb("gbo_wide", [P, P])
        gbo_row = sb("gbo_row", [P, P])
        w1 = probs[0][:, 0, GW:GW + HID].rearrange("p (m d) -> p m d", m=NH)
        w2 = probs[0][:, 1, GW:GW + HID]
        wmod = probs[0][:, 2, GW:GW + 6 * D]
        w1t_hi, w1t_lo = sb("w1t_hi", [P, HID], F32R), sb("w1t_lo", [P, HID], F32R)
        w2t_hi, w2t_lo = sb("w2t_hi", [P, HID], F32R), sb("w2t_lo", [P, HID], F32R)
        wr = sb("wr", [P, NBLK])
        wr_halves = sb("wr_halves", [P, 2, NBLK], F32R)
        br = sb("br", [P, NBLK])
        cols = sb("cols", [P, 6])
        BQ, BK, BV, BO, B2, C = range(6)
        silu = sb("silu", [P, 4])
        mod = sb("mod", [P, 6])
        SA, CA, GA, SB_, CB, GB = range(6)
        gate = sb("gate", [P, 6])
        q_bias = sb("q_bias", [P, 1])
        gbo = sb("gbo", [P, 1])
        gbb2 = sb("gbb2", [P, 1])
        ident = sb("ident", [P, P])
        ident_b = sb("ident_b", [P, P], BF16)
        causal = sb("causal", [P, P], BF16)
        pow_half = sb("pow_half", [P, GT])
        warm = sb("warm", [P, 2])
        filler = sb("filler", [P, GW], BF16)
        pick = sb("pick", [P, HID], BF16)
        route = sb("route", [P, T], BF16)
        b1 = sb("b1", [P, HID])
        b1_part = sb("b1_part", [P, HID], BF16)
        st = sb("st", [P, 2, NT, 6])
        mv = sb("mv", [P, 2, NT, 2])
        rstd = sb("rstd", [P, 2, NT])
        mean_rstd = sb("mean_rstd", [P, NT])
        cmax = sb("cmax", [P, NT, NG])
        nmax = sb("nmax", [P, NT])
        dpart = sb("dpart", [P, NT, NG])
        den = sb("den", [P, NT])
        rden = sb("rden", [P, NT])
        logit = sb("logit", [P, GT, NBLK])
        lmax = sb("lmax", [P, GT])
        ldiff = sb("ldiff", [P, GT, NBLK])
        keys = sb("keys", [P, GT, KEYS])
        top8 = sb("top8", [P, GT, 8])
        marked = sb("marked", [P, GT, KEYS])
        nmask = sb("nmask", [P, GT, NBLK], BF16)

        x_in_s = [sem(f"x_loaded{g}") for g in range(NG)]
        mod_in_s, cols_in_s, wq_in_s, wk_in_s, wv_in_s, wo_in_s = (
            sem(n) for n in ("wmod_loaded", "columns_loaded", "wq_loaded", "wk_loaded", "wv_loaded", "wo_loaded"))
        ffn_in_s, b1_in_s, b2_in_s, c_in_s = (sem(n) for n in ("ffn_weights_loaded", "b1_loaded", "b2_loaded", "c_loaded"))
        stored = [sem(f"stored{g}") for g in range(NG)]
        ident_made, causal_made, warm_made, filler_made = (
            sem(n) for n in ("ident_made", "causal_made", "warm_made", "filler_made"))
        silu_s, mod_mm, mod_ready, wv_turned, wv_t_ready = (
            sem(n) for n in ("silu_s", "mod_mm", "mod_ready", "wv_turned", "wv_t_ready"))
        u_mm, u_full_s, u_ready, rows_mm, rows_ready = (sem(n) for n in ("u_mm", "u_full_s", "u_ready", "rows_mm", "rows_ready"))
        scale_ready, qk_hi_s, qk_w_ready, bias_mm, bias_ready, wide_ready = (
            sem(n) for n in ("scale_ready", "qk_hi_s", "qk_w_ready", "bias_mm", "bias_ready", "wide_ready"))
        w_turned, w1t_hi_s, w1t_lo_s, w2t_hi_s, w2t_lo_s, ffn_w_ready, pick_ready = (
            sem(n) for n in ("w_turned", "w1t_hi_s", "w1t_lo_s", "w2t_hi_s", "w2t_lo_s", "ffn_w_ready", "pick_ready"))
        gate_ready, route_ones = sem("gate_ready"), sem("route_ones")
        stats, power_s = sem("stats"), sem("power_s")
        xn_by_act, xn_by_dve = sem("xn_by_act"), sem("xn_by_dve")
        dve_step, pool_step = sem("dve_step"), sem("pool_step")
        xt_mm, h_hi_s, h_full_s = sem("xt_mm"), sem("h_hi_s"), sem("h_full_s")
        h_lo_by_pool, h_lo_by_dve = sem("h_lo_by_pool"), sem("h_lo_by_dve")
        q_mm, k_mm, v_mm = sem("q_mm"), sem("k_mm"), sem("v_mm")
        q_hi_s, k_hi_s, v_hi_s = sem("q_hi_s"), sem("k_hi_s"), sem("v_hi_s")
        q_lo_s, k_lo_s, v_lo_s = sem("q_lo_s"), sem("k_lo_s"), sem("v_lo_s")
        xb_ready = sem("xb_ready")
        scored, nmax_ready, exp_done = sem("scored"), sem("nmax_ready"), sem("exp_done")
        turned, pt_hi_s = sem("turned"), sem("pt_hi_s")
        pt_lo_dve, pt_lo_pool, pv_done = sem("pt_lo_dve"), sem("pt_lo_pool"), sem("pv_done")
        ctx_out, ctx_turned, x1_ready = sem("ctx_out"), sem("ctx_turned"), sem("x1_ready")
        logits_mm, nmask_ready, nmask_turned, route_ready = (
            sem(n) for n in ("logits_mm", "nmask_ready", "nmask_turned", "route_ready"))
        hid_mm, hid_hi_s, hid_lo_s, y_mm, y_out, y_turned, res_ready = (
            sem(n) for n in ("hid_mm", "hid_hi_s", "hid_lo_s", "y_mm", "y_out", "y_turned", "res_ready"))

        x_tiles = x_in.rearrange("b (g i p) d -> g p (b i) d", p=P, i=GT)
        out_tiles = out.rearrange("b (g i p) d -> g p (b i) d", p=P, i=GT)
        col = lambda v: v.rearrange("(p o) -> p o", o=1)

        def grp(a, g):
            return a[:, g * GW:(g + 1) * GW]

        def tile(a, n):
            return a[:, n * P:(n + 1) * P]

        def norm_lowered(n):
            by_pool = pool_lowers(n)
            return h_lo_by_pool if by_pool else h_lo_by_dve, sum(pool_lowers(k) == by_pool for k in range(n + 1))

        def norm_applied(n):
            by_act = scalar_applies(n)
            return xn_by_act if by_act else xn_by_dve, sum(scalar_applies(k) == by_act for k in range(n + 1))

        def lower_norm(engine, n):
            engine.wait_ge(h_full_s, n + 1)
            engine.tensor_tensor(grp(h_lo, n % NG), h_full[:, n % 2, :], grp(h_hi, n % NG).bitcast(F32),
                                 ALU.subtract).then_inc(norm_lowered(n)[0], 1)

        block = ctx.enter_context(nc.Block())

        @block.sync
        def _(sp):
            def load(dst, src, done):
                sp.dma_start(dst, src).then_inc(done, 16)

            def load_x(g):
                load(x[:, g * GT:(g + 1) * GT, :], x_tiles[g], x_in_s[g])

            def on_all(v, width):
                return v.rearrange("(o n) -> o n", o=1).broadcast_to([P, width])

            load_x(0)
            load(wq[:], wq_in, wq_in_s)
            load(wk[:], wk_in, wk_in_s)
            load(wv[:], wv_in, wv_in_s)
            load_x(1)
            for n, v in ((BQ, bq_in), (BK, bk_in), (BV, bv_in)):
                load(cols[:, n:n + 1], col(v), cols_in_s)
            load(wo[:], wo_in, wo_in_s)
            load_x(2)
            load(cols[:, BO:BO + 1], col(bo_in), cols_in_s)
            load_x(3)
            load(w1, w1_in.rearrange("(m p) d -> p m d", p=P), ffn_in_s)
            load(w2, w2_in, ffn_in_s)
            load(wr[:], wr_in, ffn_in_s)
            load(br[:], on_all(br_in, NBLK), ffn_in_s)
            load(cols[:, B2:B2 + 1], col(b2_in), b2_in_s)
            load(b1[:], on_all(b1_in, HID), b1_in_s)
            for g in range(NG):
                for k, part in enumerate(result_parts(g)):
                    sp.wait_ge(res_ready, g + 1 + k)
                    sp.dma_start(out_tiles[g][:, part.start // P:part.stop // P, :],
                                 res[:, g % 2, part].rearrange("p (i d) -> p i d", d=D)).then_inc(stored[g], 16)
            for g in range(NG):
                sp.wait_ge(stored[g], 16 * len(result_parts(g)))

        @block.gpsimd
        def _(pool):
            steps = [0]

            def step(ins):
                steps[0] += 1
                ins.then_inc(pool_step, 1)
                pool.wait_ge(pool_step, steps[0])

            def power(n):
                k, s = n // NG, slice(n % NG * GT, n % NG * GT + GT)
                pool.wait_ge(stats, n + 1)
                last = pool.tensor_tensor(rstd[:, k, s], rstd[:, k, s], pow_half[:], ALU.pow)
                if scalar_applies(n):
                    step(last)
                    last = pool.tensor_tensor(mean_rstd[:, s], mean_rstd[:, s], rstd[:, k, s], ALU.mult)
                last.then_inc(power_s, 1)

            def norm_low(n):
                lower_norm(pool, n)

            def low_v(g):
                pool.wait_ge(v_hi_s, g + 1)
                pool.tensor_tensor(grp(v_lo, g), v_full[:], grp(v_hi, g).bitcast(F32),
                                   ALU.subtract).then_inc(v_lo_s, 1)

            def low_weight(lo, full, hi, done):
                pool.tensor_tensor(lo[:], full[:], hi[:].bitcast(F32), ALU.subtract).then_inc(done, 1)

            def prepare(i):
                if i == 0:
                    step(pool.memset(ident[:], 0.0))
                    step(pool.affine_select(out=ident[:], in_=ident[:], compare_op=ALU.not_equal, fill=1.0, base=0,
                                            pattern=[[-1, P]], channel_multiplier=1))
                    pool.tensor_copy(ident_b[:], ident[:]).then_inc(ident_made, 1)
                    step(pool.memset(pow_half[:], -0.5))
                elif i == 1:
                    step(pool.memset(causal[:], 0.0))
                    pool.affine_select(out=causal[:], in_=causal[:], compare_op=ALU.is_ge, fill=FAR, base=0,
                                       pattern=[[-1, P]], channel_multiplier=1).then_inc(causal_made, 1)
                elif i == 2:
                    pool.wait_ge(qk_hi_s, 1)
                    low_weight(wq_lo, wq_full, wq_hi, qk_w_ready)
                elif i == 3:
                    pool.wait_ge(qk_hi_s, 2)
                    low_weight(wk_lo, wk, wk_hi, qk_w_ready)
                elif i == 4:
                    pool.wait_ge(u_full_s, 1)
                    low_weight(u_lo, u_full, u_hi, u_ready)
                elif i == 5:
                    step(pool.memset(pick[:], 1.0))
                    step(pool.affine_select(out=pick[:], in_=pick[:], compare_op=ALU.is_ge, fill=0.0, base=0,
                                            pattern=[[1, HID]], channel_multiplier=-BLK))
                    step(pool.affine_select(out=pick[:], in_=pick[:], compare_op=ALU.is_ge, fill=0.0, base=BLK - 1,
                                            pattern=[[-1, HID]], channel_multiplier=BLK))
                elif i == 6:
                    pool.memset(keys[:], 1.0)
                    pool.memset(route[:], 1.0).then_inc(route_ones, 1)
                elif i < 7 + NG:
                    g = i - 7
                    s = slice(g * GT, (g + 1) * GT)
                    pool.wait_ge(rows_ready, 1)
                    pool.wait_ge(*norm_applied(g))
                    pool.tensor_tensor(x[:, s, :], x[:, s, :],
                                       gbo_row[:].rearrange("p (o d) -> p o d", o=1).broadcast_to([P, GT, D]),
                                       ALU.add).then_inc(xb_ready, 1)
                else:
                    k = i - 7 - NG
                    a = slice(32 + 32 * k, 33 + 32 * k)
                    if k == 0:
                        pool.wait_ge(b1_in_s, 16)
                    step(pool.tensor_copy(b1_part[:], b1[:]))
                    pool.tensor_copy(pick[a, :], b1_part[a, :]).then_inc(pick_ready, 1)
                    pool.wait_ge(pick_ready, k + 1)
                    if k < 2:
                        step(pool.tensor_tensor(b1[:], b1[:], b1_part[:], ALU.subtract))

            def key_low(t):
                s, w = t % RING, pt_cols[t]
                pool.wait_ge(pt_hi_s, t + 1)
                if t >= RING:
                    pool.wait_ge(pv_done, t - RING + 1)
                pool.tensor_tensor(pt_lo[:, s, w:], pt_full[:, splits_before(t, True) % 2, w:],
                                   pt_hi[:, s, w:].bitcast(F32), ALU.subtract).then_inc(pt_lo_pool, 1)

            run(GPSIMD_PLAN, {"z": prepare, "p": power, "n": norm_low, "v": low_v, "t": key_low})

        @block.scalar
        def _(act):
            act.dma_start(cols[:, C:C + 1], c_in.rearrange("o p -> p o")).then_inc(c_in_s, 16)
            act.dma_start(wmod, wmod_in).then_inc(mod_in_s, 16)
            act.wait_ge(warm_made, 1)
            nc.scalar.activation(warm[:, 1:2], warm[:, 0:1], ACT.Exp)

            def prepare(i):
                if i == 0:
                    act.wait_ge(c_in_s, 16)
                    nc.scalar.activation(silu[:, 0:1], cols[:, C:C + 1], ACT.Exp, scale=-1.0).then_inc(silu_s, 1)
                elif i == 1:
                    act.wait_ge(wv_turned, 1)
                    nc.scalar.copy(wv_t[:], score_bank[1][:, 0:P]).then_inc(wv_t_ready, 1)
                elif i == 2:
                    act.wait_ge(w_turned, 1)
                    nc.scalar.copy(w1t_hi[:], misc_bank[:]).then_inc(w1t_hi_s, 1)
                elif i == 3:
                    act.wait_ge(w_turned, 2)
                    nc.scalar.copy(w2t_hi[:], misc_bank[:]).then_inc(w2t_hi_s, 1)
                elif i == 4:
                    act.wait_ge(wq_in_s, 16)
                    nc.scalar.activation(wq_full[:], wq[:], ACT.Identity, scale=QSCALE)
                    nc.scalar.activation(wq_hi[:], wq[:], ACT.Identity, scale=QSCALE).then_inc(qk_hi_s, 1)
                elif i == 5:
                    act.wait_ge(wk_in_s, 16)
                    nc.scalar.copy(wk_hi[:], wk[:]).then_inc(qk_hi_s, 1)
                elif i == 6:
                    act.wait_ge(u_mm, 1)
                    nc.scalar.copy(u_full[:], score_bank[2][:, 0:P])
                    nc.scalar.copy(u_hi[:], score_bank[2][:, 0:P]).then_inc(u_full_s, 1)

            def apply(n):
                act.wait_ge(power_s, n + 1)
                if n >= 2:
                    act.wait_ge(xt_mm, n - 1)
                for i in range(GT):
                    t = n * GT + i
                    last = nc.scalar.activation(xn[:, n % 2, i, :], x[:, t, :], ACT.Identity,
                                                bias=mean_rstd[:, t:t + 1], scale=rstd[:, 0, t:t + 1])
                last.then_inc(xn_by_act, 1)

            def norm_high(n):
                act.wait_ge(xt_mm, n + 1)
                if n == 0:
                    act.wait_ge(scale_ready, 1)
                elif n == NG:
                    act.wait_ge(gate_ready, 1)
                    act.wait_ge(v_mm, NG)
                shift, scale = (SA, CA) if n < NG else (SB_, CB)
                nc.scalar.activation(grp(h_hi, n % NG), misc_bank[:], ACT.Identity, bias=mod[:, shift:shift + 1],
                                     scale=gate[:, scale:scale + 1]).then_inc(h_hi_s, 1)
                if n >= 2:
                    act.wait_ge(*norm_lowered(n - 2))
                nc.scalar.activation(h_full[:, n % 2, :], misc_bank[:], ACT.Identity, bias=mod[:, shift:shift + 1],
                                     scale=gate[:, scale:scale + 1]).then_inc(h_full_s, 1)

            def q_high(g):
                act.wait_ge(q_mm, g + 1)
                if g == 0:
                    act.wait_ge(bias_ready, 1)
                nc.scalar.activation(grp(q_hi, g), turn_bank[0][:], ACT.Identity, bias=q_bias[:]).then_inc(q_hi_s, 1)

            def k_high(g):
                act.wait_ge(k_mm, g + 1)
                if g == 0:
                    act.wait_ge(cols_in_s, 64)
                nc.scalar.activation(grp(k_hi, g), turn_bank[1][:], ACT.Identity, bias=cols[:, BK:BK + 1]).then_inc(k_hi_s, 1)

            def v_high(g):
                act.wait_ge(v_mm, g + 1)
                if g >= 1:
                    act.wait_ge(v_lo_s, g)
                nc.scalar.copy(v_full[:], ctx_bank[:])
                nc.scalar.copy(grp(v_hi, g), ctx_bank[:]).then_inc(v_hi_s, 1)

            def exps(k):
                g, r, c = chunk_of[k]
                n, w = g * GT + r, chunk_width(g, r, c)
                if c == 0:
                    act.wait_ge(nmax_ready, n + 1)
                    if r == 0 and g == 2:
                        act.wait_ge(w_turned, 2)
                        act.wait_ge(mod_mm, 2)
                    if r == 0 and g >= 2:
                        act.wait_ge(turned, key_no(g - 1, 0))
                nc.scalar.activation(probs[g % 2][:, r, c * GW:c * GW + w],
                                     score_bank[k % 4][:, 0:w], ACT.Exp, bias=nmax[:, n:n + 1],
                                     accum_out=dpart[:, n, c:c + 1]).then_inc(exp_done, 1)

            def key_high(t):
                s, w = t % RING, pt_cols[t]
                act.wait_ge(turned, t + 1)
                if pool_splits(t):
                    n = splits_before(t, True)
                    if n >= 2:
                        act.wait_ge(pt_lo_pool, n - 1)
                    nc.scalar.copy(pt_full[:, n % 2, w:], turn_bank[t % 2][:, w:])
                if t >= RING:
                    act.wait_ge(pv_done, t - RING + 1)
                nc.scalar.copy(pt_hi[:, s, w:], turn_bank[t % 2][:, w:]).then_inc(pt_hi_s, 1)

            def ctx_copy(g):
                act.wait_ge(pv_done, key_no(g + 1, 0))
                if g >= 1:
                    act.wait_ge(ctx_turned, g)
                else:
                    act.wait_ge(gate_ready, 1)
                nc.scalar.activation(ctx_sb[:], ctx_bank[:], ACT.Identity, scale=gate[:, GA:GA + 1]).then_inc(ctx_out, 1)

            def route_copy(g):
                act.wait_ge(nmask_turned, g + 1)
                if g == 0:
                    act.wait_ge(route_ones, 1)
                nc.scalar.copy(route[0:NBLK, g * GW:(g + 1) * GW],
                               misc_bank[0:NBLK, 0:GW // 2].bitcast(BF16)).then_inc(route_ready, 1)

            def hidden(n):
                g, m = n // NH, n % NH
                act.wait_ge(hid_mm, g * NH + m + 1)
                if g >= 1:
                    act.wait_ge(y_mm, (g - 1) * NH + m + 1)
                nc.scalar.activation(hid_hi[:, m, :], score_bank[(CHUNKS + g * NH + m) % 4][:], ACT.Relu).then_inc(hid_hi_s, 1)

            def y_copy(g):
                act.wait_ge(y_mm, NH * (g + 1))
                if g >= 1:
                    act.wait_ge(y_turned, g)
                for part in result_parts(g):
                    nc.scalar.activation(y_sb[:, part], turn_bank[g % 2][:, part], ACT.Identity, bias=gbb2[:],
                                         scale=gate[:, GB:GB + 1]).then_inc(y_out, 1)

            run(SCALAR_PLAN, {"z": prepare, "a": apply, "n": norm_high, "q": q_high, "k": k_high, "v": v_high, "e": exps, "t": key_high,
                              "c": ctx_copy, "m": route_copy, "h": hidden, "y": y_copy})

        @block.vector
        def _(dve):
            steps = [0]

            def step(ins):
                steps[0] += 1
                ins.then_inc(dve_step, 1)
                dve.wait_ge(dve_step, steps[0])

            def norm_stats(n):
                k, g = n // NG, n % NG
                s = slice(g * GT, (g + 1) * GT)
                if k == 0:
                    dve.wait_ge(x_in_s[g], 16)
                else:
                    dve.wait_ge(x1_ready, g + 1)
                for i in range(GT):
                    last = nc.vector.bn_stats(st[:, k, g * GT + i, :], x[:, g * GT + i, :])
                step(last)
                for i in range(GT):
                    last = nc.vector.bn_aggr(mv[:, k, g * GT + i, :], st[:, k, g * GT + i, :])
                step(last)
                if scalar_applies(n):
                    nc.vector.tensor_scalar(mean_rstd[:, s], mv[:, k, s, 0], -1.0, None, ALU.mult)
                nc.vector.tensor_scalar(rstd[:, k, s], mv[:, k, s, 1], EPS, None, ALU.add).then_inc(stats, 1)

            def apply(n):
                k, g = n // NG, n % NG
                dve.wait_ge(power_s, n + 1)
                if n >= 2:
                    dve.wait_ge(xt_mm, n - 1)
                for i in range(GT):
                    t = g * GT + i
                    last = nc.vector.tensor_scalar(xn[:, n % 2, i, :], x[:, t, :], mv[:, k, t, 0:1],
                                                   rstd[:, k, t:t + 1], ALU.subtract, ALU.mult)
                last.then_inc(xn_by_dve, 1)

            def norm_low(n):
                lower_norm(dve, n)

            def qk_low(g, n, bias, hi_s, lo_s, hi, lo):
                dve.wait_ge(hi_s, g + 1)
                nc.vector.scalar_tensor_tensor(out=grp(lo, g), in0=turn_bank[n][:], scalar=bias,
                                               in1=grp(hi, g).bitcast(F32), op0=ALU.add,
                                               op1=ALU.subtract).then_inc(lo_s, 1)

            def low_q(g):
                qk_low(g, 0, q_bias[:], q_hi_s, q_lo_s, q_hi, q_lo)

            def low_k(g):
                qk_low(g, 1, cols[:, BK:BK + 1], k_hi_s, k_lo_s, k_hi, k_lo)

            def row_max(k):
                g, r, c = chunk_of[k]
                n, w = g * GT + r, chunk_width(g, r, c)
                dve.wait_ge(scored, k + 1)
                if g == 0:
                    nc.vector.tensor_reduce(nmax[:, n:n + 1], score_bank[k % 4][:, 0:w], AX.X, ALU.max,
                                            negate=True).then_inc(nmax_ready, 1)
                    return
                last = nc.vector.tensor_reduce(cmax[:, n, c:c + 1], score_bank[k % 4][:, 0:w], AX.X, ALU.max)
                if c == g:
                    step(last)
                    nc.vector.tensor_reduce(nmax[:, n:n + 1], cmax[:, n, 0:g + 1], AX.X, ALU.max,
                                            negate=True).then_inc(nmax_ready, 1)

            def key_low(t):
                s, w = t % RING, pt_cols[t]
                dve.wait_ge(pt_hi_s, t + 1)
                if t >= RING:
                    dve.wait_ge(pv_done, t - RING + 1)
                nc.vector.tensor_tensor(pt_lo[:, s, w:], turn_bank[t % 2][:, w:], pt_hi[:, s, w:].bitcast(F32),
                                        ALU.subtract).then_inc(pt_lo_dve, 1)

            def row_sums(g):
                s = slice(g * GT, (g + 1) * GT)
                dve.wait_ge(exp_done, chunk_no(g + 1, 0, 0))
                step(nc.vector.tensor_reduce(den[:, s], dpart[:, s, 0:g + 1], AX.X, ALU.add))
                step(nc.vector.reciprocal(rden[:, s], den[:, s]))

            def attention_out(g):
                row_sums(g)
                dve.wait_ge(ctx_turned, g + 1)
                dve.wait_ge(xb_ready, g + 1)
                for i in range(GT):
                    t = g * GT + i
                    last = nc.vector.scalar_tensor_tensor(out=x[:, t, :], in0=tile(misc_bank, i),
                                                          scalar=rden[:, t:t + 1], in1=x[:, t, :],
                                                          op0=ALU.mult, op1=ALU.add)
                last.then_inc(x1_ready, 1)
                norm_stats(NG + g)

            def choose(g):
                dve.wait_ge(logits_mm, g + 1)
                if g == 0:
                    dve.wait_ge(route_ones, 1)
                sums = misc_bank[:, 0:GT * 2 * NBLK].rearrange("p (i s e) -> p i s e", i=GT, s=2)
                step(nc.vector.tensor_tensor(logit[:], sums[:, :, 1, :],
                                             br[:].rearrange("p (o e) -> p o e", o=1).broadcast_to([P, GT, NBLK]),
                                             ALU.add))
                step(nc.vector.tensor_tensor(logit[:], sums[:, :, 0, :], logit[:], ALU.add))
                step(nc.vector.tensor_reduce(lmax[:], logit[:], AX.X, ALU.max))
                step(nc.vector.tensor_tensor(ldiff[:], logit[:],
                                             lmax[:].rearrange("p (i o) -> p i o", o=1).broadcast_to([P, GT, NBLK]),
                                             ALU.subtract))
                step(nc.vector.tensor_scalar(keys[:, :, 0:NBLK], ldiff[:], UNDER, None, ALU.max))
                for i in range(GT):
                    last = nc.vector.max(top8[:, i, :], keys[:, i, :])
                step(last)
                for i in range(GT):
                    last = nc.vector.match_replace(marked[:, i, :], top8[:, i, :], keys[:, i, :], 1.0)
                step(last)
                if g >= 1:
                    dve.wait_ge(nmask_turned, g)
                nc.vector.tensor_scalar(nmask[:], marked[:, :, 0:NBLK], 0.0, FAR, ALU.is_le, ALU.mult).then_inc(nmask_ready, 1)

            def hidden(n):
                g, m = n // NH, n % NH
                dve.wait_ge(hid_hi_s, n + 1)
                if g >= 1:
                    dve.wait_ge(y_mm, (g - 1) * NH + m + 1)
                nc.vector.scalar_tensor_tensor(out=hid_lo[:, m, :], in0=score_bank[(CHUNKS + n) % 4][:], scalar=0.0,
                                               in1=hid_hi[:, m, :].bitcast(F32), op0=ALU.max,
                                               op1=ALU.subtract).then_inc(hid_lo_s, 1)

            def finish(g):
                if g >= 2:
                    dve.wait_ge(stored[g - 2], 16)
                for k, part in enumerate(result_parts(g)):
                    dve.wait_ge(y_turned, g + 1 + k)
                    nc.vector.tensor_tensor(res[:, g % 2, part], result_bank[k][:, part],
                                            x[:, g * GT:(g + 1) * GT, :].rearrange("p i d -> p (i d)")[:, part],
                                            ALU.add).then_inc(res_ready, 1)

            def prepare(i):
                if i == 0:
                    dve.wait_ge(silu_s, 1)
                    step(nc.vector.tensor_scalar(silu[:, 1:2], silu[:, 0:1], 1.0, None, ALU.add))
                    step(nc.vector.reciprocal(silu[:, 2:3], silu[:, 1:2]))
                    nc.vector.tensor_tensor(silu[:, 3:4], silu[:, 2:3], cols[:, C:C + 1], ALU.mult).then_inc(silu_s, 1)
                elif i == 1:
                    dve.wait_ge(mod_mm, 1)
                    nc.vector.tensor_copy(mod[:, 0:2], score_bank[0][:, 0:2])
                    nc.vector.tensor_scalar(gate[:, CA:CA + 1], score_bank[0][:, CA:CA + 1], 1.0, None,
                                            ALU.add).then_inc(scale_ready, 1)
                elif i == 4:
                    nc.vector.tensor_scalar(gate[:, CB:CB + 1], mod[:, CB:CB + 1], 1.0, None, ALU.add)
                    for s, sign in ((GA, SA), (GB, SB_)):
                        last = nc.vector.tensor_scalar(gate[:, sign:sign + 1], mod[:, s:s + 1], 0.0, 2.0,
                                                       ALU.is_ge, ALU.mult)
                    step(last)
                    for s, sign in ((GA, SA), (GB, SB_)):
                        last = nc.vector.tensor_scalar(gate[:, sign:sign + 1], gate[:, sign:sign + 1], -1.0, None, ALU.add)
                    step(last)
                    for s, sign in ((GA, SA), (GB, SB_)):
                        last = nc.vector.tensor_scalar(gate[:, s:s + 1], mod[:, s:s + 1], gate[:, sign:sign + 1], 0.25,
                                                       ALU.mult, ALU.max)
                    step(last)
                    for s, sign in ((GA, SA), (GB, SB_)):
                        last = nc.vector.tensor_scalar(gate[:, s:s + 1], gate[:, s:s + 1], gate[:, sign:sign + 1], None,
                                                       ALU.mult)
                    step(last)
                    dve.wait_ge(b2_in_s, 16)
                    nc.vector.tensor_scalar(gbb2[:], gate[:, GB:GB + 1], cols[:, B2:B2 + 1], None,
                                            ALU.mult).then_inc(gate_ready, 1)
                elif i == 5:
                    dve.wait_ge(cols_in_s, 64)
                    nc.vector.tensor_scalar(q_bias[:], cols[:, BQ:BQ + 1], QSCALE, None, ALU.mult).then_inc(bias_ready, 1)
                elif i == 7:
                    dve.wait_ge(bias_mm, 1)
                    step(nc.vector.tensor_scalar(gbo[:], misc_bank[:, 0:1], cols[:, BO:BO + 1],
                                                 gate[:, GA:GA + 1], ALU.add, ALU.mult))
                    dve.wait_ge(ident_made, 1)
                    nc.vector.tensor_scalar(gbo_wide[:], ident[:], 0.0, gbo[:], ALU.mult, ALU.add).then_inc(wide_ready, 1)
                elif i == 8:
                    dve.wait_ge(w1t_hi_s, 1)
                    nc.vector.tensor_tensor(w1t_lo[:], misc_bank[:], w1t_hi[:].bitcast(F32),
                                            ALU.subtract).then_inc(w1t_lo_s, 1)
                elif i == 9:
                    dve.wait_ge(w2t_hi_s, 1)
                    nc.vector.tensor_tensor(w2t_lo[:], misc_bank[:], w2t_hi[:].bitcast(F32),
                                            ALU.subtract).then_inc(w2t_lo_s, 1)
                    dve.wait_ge(ffn_in_s, 64)
                    step(nc.vector.tensor_copy(wr_halves[:, 0, :], wr[:]))
                    nc.vector.tensor_tensor(wr_halves[:, 1, :], wr[:], wr_halves[:, 0, :].bitcast(F32),
                                            ALU.subtract).then_inc(ffn_w_ready, 1)
                elif i == 10:
                    dve.wait_ge(rows_mm, 1)
                    nc.vector.tensor_copy(gbo_row[:], misc_bank[:, 0:P]).then_inc(rows_ready, 1)
                elif i == 12:
                    dve.wait_ge(mod_mm, 2)
                    nc.vector.tensor_copy(mod[:, 2:6], ctx_bank[:, 2:6]).then_inc(mod_ready, 1)
                    dve.wait_ge(mod_ready, 1)

            nc.vector.memset(filler[:], 0.0).then_inc(filler_made, 1)
            nc.vector.memset(warm[:, 0:1], 0.0).then_inc(warm_made, 1)
            run(VECTOR_PLAN, {"z": prepare, "g": norm_stats, "a": apply, "n": norm_low, "q": low_q, "k": low_k, "s": row_max,
                              "t": key_low, "x": attention_out, "m": choose, "h": hidden, "f": finish})

        @block.tensor
        def _(pe):
            mm = nc.tensor.matmul

            def three(dst, w_hi, w_lo, m_hi, m_lo, hi_wait=None, lo_wait=None, start=True, stop=True):
                if hi_wait:
                    pe.wait_ge(*hi_wait)
                mm(dst, w_hi, m_hi, start=start, stop=False)
                mm(dst, w_lo, m_hi, start=False, stop=False)
                if lo_wait:
                    pe.wait_ge(*lo_wait)
                return mm(dst, w_hi, m_lo, start=False, stop=stop)

            def turn_norm(n):
                pe.wait_ge(*norm_applied(n))
                if n == 0:
                    pe.wait_ge(ident_made, 1)
                elif n == NG - 1:
                    pe.wait_ge(rows_ready, 1)
                elif n < NG:
                    pe.wait_ge(h_full_s, n)
                else:
                    pe.wait_ge(x1_ready, n - NG + 1)
                for i in range(GT):
                    last = nc.tensor.transpose(tile(misc_bank, i), xn[:, n % 2, i, :], ident[:])
                last.then_inc(xt_mm, 1)

            def turn_bank_free(t):
                if pool_splits(t):
                    pe.wait_ge(pt_hi_s, t + 1)
                else:
                    pe.wait_ge(pt_lo_dve, splits_before(t, False) + 1)

            def project_q(g):
                pe.wait_ge(qk_w_ready, 1)
                if g == NG - 1:
                    turn_bank_free(LATE)
                elif g >= 1:
                    pe.wait_ge(q_lo_s, g)
                three(turn_bank[0][:], wq_hi[:], wq_lo[:], grp(h_hi, g), grp(h_lo, g),
                      (h_hi_s, g + 1), norm_lowered(g)).then_inc(q_mm, 1)

            def project_k(g):
                pe.wait_ge(qk_w_ready, 2)
                if g == NG - 1:
                    turn_bank_free(LATE + 1)
                elif g >= 1:
                    pe.wait_ge(k_lo_s, g)
                three(turn_bank[1][:], wk_hi[:], wk_lo[:], grp(h_hi, g), grp(h_lo, g),
                      (h_hi_s, g + 1), norm_lowered(g)).then_inc(k_mm, 1)

            def project_v(g):
                pe.wait_ge(*norm_lowered(g))
                if g == 0:
                    pe.wait_ge(u_ready, 1)
                    pe.wait_ge(mod_ready, 1)
                elif g < NG - 1:
                    pe.wait_ge(v_hi_s, g)
                else:
                    pe.wait_ge(ctx_out, 1)
                for n in range(g * GT, (g + 1) * GT):
                    last = three(tile(ctx_bank, n % GT), tile(h_hi, n), tile(h_lo, n), u_hi[:], u_lo[:])
                last.then_inc(v_mm, 1)

            def score(k):
                g, r, c = chunk_of[k]
                w, t = chunk_width(g, r, c), g * GT + r
                if k == 0:
                    pe.wait_ge(causal_made, 1)
                elif k == 1:
                    pe.wait_ge(wv_t_ready, 1)
                elif k == 2:
                    pe.wait_ge(u_full_s, 1)
                if k >= 4:
                    pe.wait_ge(exp_done, k - 3)
                if c == 0 and r == 0:
                    pe.wait_ge(q_lo_s, g + 1)
                    pe.wait_ge(k_lo_s, g + 1)
                last = three(score_bank[k % 4][:, 0:w], tile(q_hi, t), tile(q_lo, t), k_hi[:, c * GW:c * GW + w],
                             k_lo[:, c * GW:c * GW + w], stop=(c < g))
                if c == g:
                    last = mm(score_bank[k % 4][:, w - P:w], ident_b[:], causal[:], start=False, stop=True)
                last.then_inc(scored, 1)

            def turn_keys(t):
                g, j = key_of[t]
                pe.wait_ge(exp_done, chunk_no(g, GT - 1, j // GT) + 1)
                if t < 2:
                    pe.wait_ge((q_lo_s, k_lo_s)[t], NG - 1)
                elif LATE + 2 <= t < LATE + 4:
                    pe.wait_ge((q_lo_s, k_lo_s)[t - LATE - 2], NG)
                else:
                    turn_bank_free(t - 2)
                for r in range(key_from(g, j), GT):
                    last = nc.tensor.transpose(turn_bank[t % 2][:, r * P:(r + 1) * P],
                                               probs[g % 2][:, r, j * P:(j + 1) * P], ident[:])
                last.then_inc(turned, 1)

            def weigh(t):
                g, j = key_of[t]
                last_j = GT * (g + 1) - 1
                s, w = t % RING, pt_cols[t]
                by_pool = pool_splits(t)
                if j == 0:
                    if g == 0:
                        pe.wait_ge(v_lo_s, NG - 1)
                    elif g == 1:
                        pe.wait_ge(v_hi_s, NG)
                    else:
                        pe.wait_ge(v_lo_s, NG)
                        pe.wait_ge(ctx_out, g)
                three(ctx_bank[:, w:], tile(v_hi, j), tile(v_lo, j), pt_hi[:, s, w:], pt_lo[:, s, w:],
                      (pt_hi_s, t + 1), (pt_lo_pool if by_pool else pt_lo_dve, splits_before(t, by_pool) + 1),
                      start=(j == 0), stop=(j == last_j)).then_inc(pv_done, 1)

            def turn_context(g):
                pe.wait_ge(ctx_out, g + 1)
                if g == 0:
                    pe.wait_ge(h_full_s, NG)
                else:
                    pe.wait_ge(route_ready, g)
                for i in range(GT):
                    last = nc.tensor.transpose(tile(misc_bank, i), tile(ctx_sb, i), ident[:])
                last.then_inc(ctx_turned, 1)

            def router(g):
                pe.wait_ge(*norm_lowered(NG + g))
                if g == 0:
                    pe.wait_ge(ffn_w_ready, 1)
                for i in range(GT):
                    sums = misc_bank[:, i * 2 * NBLK:(i + 1) * 2 * NBLK]
                    halves = wr_halves[:].rearrange("p s e -> p (s e)")
                    mm(sums, tile(h_hi, g * GT + i), halves, start=True, stop=False)
                    last = mm(sums, tile(h_lo, g * GT + i), halves, start=False, stop=True)
                last.then_inc(logits_mm, 1)

            def turn_mask(g):
                pe.wait_ge(nmask_ready, g + 1)
                for i in range(GT):
                    last = nc.tensor.transpose(misc_bank[0:NBLK, i * P // 2:(i + 1) * P // 2].bitcast(BF16),
                                               nmask[:, i, :], ident_b[:])
                last.then_inc(nmask_turned, 1)

            def hidden(n):
                g, m = n // NH, n % NH
                if n < 4:
                    pe.wait_ge(exp_done, CHUNKS - 3 + n)
                else:
                    pe.wait_ge(hid_lo_s, n - 3)
                if n == 0:
                    pe.wait_ge(pick_ready, 3)
                if m == 0:
                    pe.wait_ge(route_ready, g + 1)
                    pe.wait_ge(*norm_lowered(NG + g))
                dst = score_bank[(CHUNKS + n) % 4][:]
                three(dst, tile(w1t_hi, m), tile(w1t_lo, m), grp(h_hi, g), grp(h_lo, g), stop=False)
                mm(dst, tile(pick, m), grp(route, g), start=False, stop=True).then_inc(hid_mm, 1)

            def down(n):
                g, m = n // NH, n % NH
                if m == 0:
                    if g < 2:
                        pe.wait_ge(pt_lo_dve, splits_before(len(pt_cols), False))
                        pe.wait_ge(pt_hi_s, len(pt_cols))
                    else:
                        pe.wait_ge(y_out, g - 1)
                three(turn_bank[g % 2][:], tile(w2t_hi, m), tile(w2t_lo, m), hid_hi[:, m, :], hid_lo[:, m, :],
                      (hid_hi_s, n + 1), (hid_lo_s, n + 1), start=(m == 0), stop=(m == NH - 1)).then_inc(y_mm, 1)

            def turn_y(g):
                if g == 0:
                    pe.wait_ge(ctx_out, NG)
                else:
                    pe.wait_ge(res_ready, g)
                for k, part in enumerate(result_parts(g)):
                    pe.wait_ge(y_out, g + 1 + k)
                    for i in range(part.start // P, part.stop // P):
                        last = nc.tensor.transpose(tile(result_bank[k], i), tile(y_sb, i), ident[:])
                    last.then_inc(y_turned, 1)

            def turn_weight(w):
                for m in range(NH):
                    last = nc.tensor.transpose(tile(misc_bank, m), w(m), ident[:])
                last.then_inc(w_turned, 1)

            def modulate(dst, lo, hi):
                for n in range(lo, hi):
                    last = mm(dst[:, n:n + 1], tile(wmod, n), silu[:, 3:4], start=True, stop=True)
                last.then_inc(mod_mm, 1)

            def prepare(i):
                if i == 0:
                    pe.wait_ge(ident_made, 1)
                    pe.wait_ge(wv_in_s, 16)
                    nc.tensor.transpose(score_bank[1][:, 0:P], wv[:], ident[:]).then_inc(wv_turned, 1)
                elif i == 1:
                    pe.wait_ge(silu_s, 2)
                    pe.wait_ge(mod_in_s, 16)
                    modulate(score_bank[0], 0, 2)
                elif i == 2:
                    modulate(ctx_bank, 2, 6)
                elif i == 3:
                    pe.wait_ge(wo_in_s, 16)
                    pe.wait_ge(wv_t_ready, 1)
                    mm(score_bank[2][:, 0:P], wv_t[:], wo[:], start=True, stop=True).then_inc(u_mm, 1)
                elif i == 5:
                    pe.wait_ge(cols_in_s, 64)
                    pe.wait_ge(h_full_s, NG - 1)
                    mm(misc_bank[:, 0:1], wo[:], cols[:, BV:BV + 1], start=True, stop=True).then_inc(bias_mm, 1)
                elif i == 6:
                    pe.wait_ge(ffn_in_s, 64)
                    pe.wait_ge(wide_ready, 1)
                    turn_weight(lambda m: w1[:, m, :])
                elif i == 7:
                    pe.wait_ge(w1t_lo_s, 1)
                    turn_weight(lambda m: tile(w2, m))
                elif i == 8:
                    pe.wait_ge(w2t_lo_s, 1)
                    mm(misc_bank[:, 0:P], gbo_wide[:], ident[:], start=True, stop=True).then_inc(rows_mm, 1)

            def wake(i):
                mm(score_bank[3][:, 0:GW // 2], filler[:, 0:P], filler[:, 0:GW // 2], start=True, stop=True)

            pe.wait_ge(filler_made, 1)
            for _ in range(WAKE):
                mm(score_bank[3][:], filler[:, 0:P], filler[:], start=True, stop=True)
            run(TENSOR_PLAN, {"i": wake, "z": prepare, "n": turn_norm, "q": project_q, "k": project_k, "v": project_v, "s": score,
                              "t": turn_keys, "w": weigh, "c": turn_context, "r": router, "m": turn_mask,
                              "h": hidden, "d": down, "y": turn_y})


_INS = ['L0_attn_y_all', 'L0_attn_Wq', 'L0_attn_bq', 'L0_attn_Wk', 'L0_attn_bk', 'L0_attn_Wv', 'L0_attn_bv',
        'L0_attn_Wo', 'L0_attn_bo', 'L0_ffn_w_router', 'L0_ffn_b_router', 'L0_ffn_w1', 'L0_ffn_b1', 'L0_ffn_w2',
        'L0_ffn_b2', 'L0_c', 'L0_wmod']
_OUTS = [((1, 2048, 128), 'float32')]


def kernel(**inputs):
    import numpy as _np
    import concourse.bacc as _bacc
    from concourse import mybir as _mybir
    from concourse.bass_utils import run_bass_kernel_spmd as _run

    nc = _bacc.Bacc("TRN2", target_bir_lowering=False, num_devices=1)
    arrays, args = {}, []
    for name in _INS:
        a = _np.ascontiguousarray(inputs[name])
        arrays[f"in_{name}_dram"] = a
        args.append(nc.dram_tensor(f"in_{name}_dram", a.shape, _mybir.dt.from_np(a.dtype), kind="ExternalInput").ap())
    for i, (shape, dtype) in enumerate(_OUTS):
        dt = _mybir.dt.from_np(_np.dtype(dtype))
        args.append(nc.dram_tensor(f"out_{i}_dram", shape, dt, kind="ExternalOutput").ap())
    adaln_attention_sparse_ffn(nc, *args)
    r = _run(nc, [arrays], core_ids=[0])
    got = tuple(r.results[0][f"out_{i}_dram"] for i in range(len(_OUTS)))
    return got[0]
```
